# Optimizing a Trainium2 kernel written in Bass

```python
import numpy as np
import jax
import jax.numpy as jnp

def _softmax(x, axis=-1):
    return jax.nn.softmax(x, axis=axis)

def _gelu(x):
    return jax.nn.gelu(x, approximate=True)

def _silu(x):
    return jax.nn.silu(x)

def _sigmoid(x):
    return jax.nn.sigmoid(x)

def _layernorm(x, axis=-1, eps=1e-05):
    m = jnp.mean(x, axis=axis, keepdims=True)
    v = jnp.var(x, axis=axis, keepdims=True)
    return (x - m) / jnp.sqrt(v + eps)

def _scatter_add(tgt, idx, src, axis=0):
    return tgt.at[idx].add(src)

def _segment_sum(src, seg, n):
    return jax.ops.segment_sum(src, seg, n)
kernel_name = 'mk_decoder_postln_d1_seqx_r8_6a2b5c'

def setup_inputs(seed: int=0):
    np.random.seed(seed)
    _w = jnp.asarray

    def _rec_inputs():
        import jax
        import jax.numpy as jnp
        _rk = jax.random.key(seed)
        x = -0.0005207 + 1.001 * jax.random.normal(jax.random.fold_in(_rk, 1), (32, 64, 128), jnp.float32)
        _lenS = 64 - jax.random.randint(jax.random.fold_in(_rk, 7), (32,), 0, max(1, 64 // 4) + 1, jnp.int32)
        _lenS2 = 64 - jax.random.randint(jax.random.fold_in(_rk, 8), (32,), 0, max(1, 64 // 4) + 1, jnp.int32)
        _ctx_512P = jax.random.normal(jax.random.fold_in(_rk, 11), (32, 16, 64), jnp.float32)
        _ctx_512c = jax.random.dirichlet(jax.random.fold_in(_rk, 511), 0.3 * jnp.ones((16,), jnp.float32), (32, 64))
        _ctx_512t = jnp.einsum('bsk,bkd->bsd', _ctx_512c, _ctx_512P)
        _ctx_512t = _ctx_512t * jax.lax.rsqrt(jnp.mean(jnp.square(_ctx_512t)) + 1e-12) * 0.953939
        ctx_512 = 0.502058 + 0.29099 * (_ctx_512t + 0.3 * jax.random.normal(jax.random.fold_in(_rk, 611), (32, 64, 64), jnp.float32))
        itok_BxS2xS_0_7 = jax.random.randint(jax.random.fold_in(_rk, 12), (32, 64, 64), 0, 8, jnp.int32)
        return (x, ctx_512, itok_BxS2xS_0_7)
    x, ctx_512, itok_BxS2xS_0_7 = _rec_inputs()

    def _L0_attn_setup():
        import jax, jax.numpy as jnp
        import numpy as np
        B, L, H, N = (8, 512, 128, 32)

        def _s4d_kernel(log_dt, A_real, A_imag, C_real, C_imag, seq_len):
            dt = jnp.exp(log_dt)[:, None]
            A = -jnp.exp(A_real) + 1j * A_imag
            dtA = A * dt
            C = (C_real + 1j * C_imag) * (jnp.exp(dtA) - 1.0) / A
            vand = jnp.exp(dtA[:, :, None] * jnp.arange(seq_len, dtype=jnp.float32))
            return 2.0 * jnp.einsum('hn,hnl->hl', C, vand).real
        key = jax.random.key(seed)
        k0, k1, k2, k3 = jax.random.split(key, 4)
        u = jax.random.normal(k0, (B, L, H), jnp.float32)
        log_dt = jnp.log(0.001) + jax.random.uniform(k1, (H,), jnp.float32) * (jnp.log(0.1) - jnp.log(0.001))
        A_real = jnp.full((H, N), jnp.log(0.5), jnp.float32)
        A_imag = jnp.broadcast_to(jnp.pi * jnp.arange(N, dtype=jnp.float32), (H, N))
        C_real = jax.random.normal(k2, (H, N), jnp.float32) * 0.5 ** 0.5
        C_imag = jax.random.normal(k3, (H, N), jnp.float32) * 0.5 ** 0.5
        D = jnp.asarray(0.0, jnp.float32)
        return dict(u=u, log_dt=log_dt, A_real=A_real, A_imag=A_imag, C_real=C_real, C_imag=C_imag, D=D)
    _L0_attn_all = _L0_attn_setup()
    _L0_attn_in = {k: v for k, v in _L0_attn_all.items() if k in ('log_dt', 'A_real', 'A_imag', 'C_real', 'C_imag', 'D')}
    del _L0_attn_all

    def _L0_xattn_setup():
        import jax, jax.numpy as jnp
        import numpy as np
        key = jax.random.key(seed)
        k1, k2, k3, k4, k5 = jax.random.split(key, 5)
        B, K, S, E, I, D = (4, 2, 64, 8, 128, 256)
        x = jax.random.normal(k1, (B, S, I), dtype=jnp.float32)
        weights = jax.random.uniform(k2, (B, K, S), dtype=jnp.float32)
        ensembles = jax.random.randint(k3, (B, K, S), 0, E, dtype=jnp.int64)
        lim1 = float(np.sqrt(6.0 / (D + I)))
        proj_in = jax.random.uniform(k4, (E, D, I), dtype=jnp.float32, minval=-lim1, maxval=lim1)
        proj_out = jax.random.uniform(k5, (E, I, D), dtype=jnp.float32, minval=-lim1, maxval=lim1)
        return {'x': x, 'weights': weights, 'ensembles': ensembles, 'proj_in': proj_in, 'proj_out': proj_out}
    _L0_xattn_all = _L0_xattn_setup()
    _L0_xattn_in = {k: v for k, v in _L0_xattn_all.items() if k in ('proj_in', 'proj_out')}
    del _L0_xattn_all

    def _L0_ffn_setup():
        import jax, jax.numpy as jnp
        import numpy as np
        B, S, D_MODEL, D_FF = (4, 256, 128, 512)

        def _quantum_transform(hidden, theta, w_real, w_imag):
            imag = w_imag * jnp.sin(theta + hidden * 0.1)
            quantum_phase = jnp.cos(theta) * w_real + jnp.sin(theta) * w_imag
            return hidden + quantum_phase * imag * 0.1
        key = jax.random.key(seed)
        ks = jax.random.split(key, 8)
        return {'x': jax.random.normal(ks[0], (B, S, D_MODEL), dtype=jnp.float32), 'W1': jax.random.normal(ks[1], (D_MODEL, D_FF), dtype=jnp.float32) * (1.0 / np.sqrt(D_MODEL)), 'b1': jnp.zeros((D_FF,), dtype=jnp.float32), 'quantum_phases': jax.random.normal(ks[2], (D_FF,), dtype=jnp.float32) * (2.0 * np.pi), 'quantum_weights_real': jax.random.normal(ks[3], (D_FF,), dtype=jnp.float32) * 0.1, 'quantum_weights_imag': jax.random.normal(ks[4], (D_FF,), dtype=jnp.float32) * 0.1, 'W2': jax.random.normal(ks[5], (D_FF, D_MODEL), dtype=jnp.float32) * (1.0 / np.sqrt(D_FF)), 'b2': jnp.zeros((D_MODEL,), dtype=jnp.float32)}
    _L0_ffn_all = _L0_ffn_setup()
    _L0_ffn_in = {k: v for k, v in _L0_ffn_all.items() if k in ('W1', 'b1', 'quantum_phases', 'quantum_weights_real', 'quantum_weights_imag', 'W2', 'b2')}
    del _L0_ffn_all
    return {'x': x, 'ctx_512': ctx_512, 'itok_BxS2xS_0_7': itok_BxS2xS_0_7, 'L0_attn_log_dt': _L0_attn_in['log_dt'], 'L0_attn_A_real': _L0_attn_in['A_real'], 'L0_attn_A_imag': _L0_attn_in['A_imag'], 'L0_attn_C_real': _L0_attn_in['C_real'], 'L0_attn_C_imag': _L0_attn_in['C_imag'], 'L0_attn_D': _L0_attn_in['D'], 'L0_xattn_proj_in': _L0_xattn_in['proj_in'], 'L0_xattn_proj_out': _L0_xattn_in['proj_out'], 'L0_ffn_W1': _L0_ffn_in['W1'], 'L0_ffn_b1': _L0_ffn_in['b1'], 'L0_ffn_quantum_phases': _L0_ffn_in['quantum_phases'], 'L0_ffn_quantum_weights_real': _L0_ffn_in['quantum_weights_real'], 'L0_ffn_quantum_weights_imag': _L0_ffn_in['quantum_weights_imag'], 'L0_ffn_W2': _L0_ffn_in['W2'], 'L0_ffn_b2': _L0_ffn_in['b2']}

def reference(x, ctx_512, itok_BxS2xS_0_7, L0_attn_log_dt, L0_attn_A_real, L0_attn_A_imag, L0_attn_C_real, L0_attn_C_imag, L0_attn_D, L0_xattn_proj_in, L0_xattn_proj_out, L0_ffn_W1, L0_ffn_b1, L0_ffn_quantum_phases, L0_ffn_quantum_weights_real, L0_ffn_quantum_weights_imag, L0_ffn_W2, L0_ffn_b2):
    import jax
    import jax.numpy as jnp

    def _L0_attn_ref(u, log_dt, A_real, A_imag, C_real, C_imag, D):
        import jax, jax.numpy as jnp
        import numpy as np
        B, L, H, N = (8, 512, 128, 32)

        def _s4d_kernel(log_dt, A_real, A_imag, C_real, C_imag, seq_len):
            dt = jnp.exp(log_dt)[:, None]
            A = -jnp.exp(A_real) + 1j * A_imag
            dtA = A * dt
            C = (C_real + 1j * C_imag) * (jnp.exp(dtA) - 1.0) / A
            vand = jnp.exp(dtA[:, :, None] * jnp.arange(seq_len, dtype=jnp.float32))
            return 2.0 * jnp.einsum('hn,hnl->hl', C, vand).real
        seq_len = u.shape[1]
        K = _s4d_kernel(log_dt, A_real, A_imag, C_real, C_imag, seq_len)
        n_fft = 2 * seq_len
        u_f = jnp.fft.rfft(u, n=n_fft, axis=1)
        k_f = jnp.fft.rfft(K, n=n_fft, axis=-1).T
        y = jnp.fft.irfft(u_f * k_f[None], n=n_fft, axis=1)[:, :seq_len]
        y = y + D * u
        return jax.nn.gelu(y, approximate=False)

    def _L0_xattn_ref(x, weights, ensembles, proj_in, proj_out):
        import jax, jax.numpy as jnp
        import numpy as np
        E = proj_in.shape[0]
        h = jax.nn.relu(jnp.einsum('edi,bsi->bsed', proj_in, x))
        o = jnp.einsum('eid,bsed->bsei', proj_out, h)
        onehot = jax.nn.one_hot(ensembles, E, dtype=x.dtype)
        gate = jnp.einsum('bks,bkse->bse', weights, onehot)
        return jnp.einsum('bsei,bse->bsi', o, gate)

    def _L0_ffn_ref(x, W1, b1, quantum_phases, quantum_weights_real, quantum_weights_imag, W2, b2):
        import jax, jax.numpy as jnp
        import numpy as np
        B, S, D_MODEL, D_FF = (4, 256, 128, 512)

        def _quantum_transform(hidden, theta, w_real, w_imag):
            imag = w_imag * jnp.sin(theta + hidden * 0.1)
            quantum_phase = jnp.cos(theta) * w_real + jnp.sin(theta) * w_imag
            return hidden + quantum_phase * imag * 0.1
        hidden = jnp.einsum('bsd,df->bsf', x, W1) + b1
        q = _quantum_transform(hidden, quantum_phases, quantum_weights_real, quantum_weights_imag)
        act = jax.nn.relu(q)
        return jnp.einsum('bsf,fd->bsd', act, W2) + b2
    x = _layernorm(x + _L0_attn_ref(x, L0_attn_log_dt, L0_attn_A_real, L0_attn_A_imag, L0_attn_C_real, L0_attn_C_imag, L0_attn_D), axis=-1)
    x = _layernorm(x + _L0_xattn_ref(x, ctx_512, itok_BxS2xS_0_7, L0_xattn_proj_in, L0_xattn_proj_out), axis=-1)
    x = _layernorm(x + _L0_ffn_ref(x, L0_ffn_W1, L0_ffn_b1, L0_ffn_quantum_phases, L0_ffn_quantum_weights_real, L0_ffn_quantum_weights_imag, L0_ffn_W2, L0_ffn_b2), axis=-1)
    return x

_drawn_inputs = setup_inputs


def setup_inputs(seed=0):
    import zlib

    import numpy as np

    out = dict(_drawn_inputs(seed))
    spreads = {'L0_attn_A_real': (-0.6931471824645996, 0.6),
     'L0_ffn_b1': (0.0, 0.1),
     'L0_ffn_b2': (0.0, 0.1)}
    factors = {'L0_ffn_quantum_phases': 8.0,
     'L0_ffn_quantum_weights_real': 34.969,
     'L0_ffn_quantum_weights_imag': 8.0}
    for name, (base, spread) in spreads.items():
        noise = np.random.default_rng([zlib.crc32(name.encode()), seed]).standard_normal(out[name].shape)
        drawn = base * np.exp(spread * noise) if base else spread * noise
        out[name] = jnp.asarray(drawn.astype(out[name].dtype))
    for name, factor in factors.items():
        out[name] = (out[name] * factor).astype(out[name].dtype)
    return out
```

```python
from contextlib import ExitStack

import concourse.bass as bass
from concourse import mybir

F32 = mybir.dt.float32
F32R = mybir.dt.float32r
I32 = mybir.dt.int32
ALU = mybir.AluOpType
ACT = mybir.ActivationFunctionType
AX_X = mybir.AxisListType.X

P = 128
TWO_PI_HI = 6.28125
TWO_PI_LO = 0.0019353071795864769
INV_TWO_PI = 0.15915494309189535
ROUND = 12582912.0
PI_BELOW = 3.1415925
TWO_PI_BELOW = 6.283185
EPS = 1e-5


def view(ap, dims, shift=0):
    return bass.AP(ap.tensor, ap.offset + shift, [list(ap.ap[0])] + [list(d) for d in dims])


def s4d_moe_ffn_decoder(nc, x, gate_w, gate_id, log_dt, a_real, a_imag, c_real, c_imag, d_skip,
                        w_in, w_out, w1, b1, theta, q_real, q_imag, w2, b2, kpad, gates, out):
    B, L, H = x.shape
    N = a_real.shape[1]
    E, D, _ = w_in.shape
    F = w1.shape[1]
    T = B * L
    PAIR = P // L
    C = B // PAIR
    GT = 512
    G = T // GT
    TG = GT // P
    DH = D // P
    NB = E * DH
    FB = F // P
    HC = H // G
    LAG = 3
    RING = 4
    ROWS = L // 8
    assert H == P and GT == 4 * P and L == 64 and FB == 4 and NB == 16 and G == 4

    with ExitStack() as ctx:
        def sb(name, shape, dt=F32):
            return ctx.enter_context(nc.sbuf_tensor(name, shape, dt))

        def sem(name):
            return ctx.enter_context(nc.semaphore(name))

        CH = HC * P
        big = sb("big", [P, G * CH])
        toep = big[:, :].rearrange("p (h l) -> p h l", l=P)
        prod = big[:, 0:CH]
        win_raw = big[:, 3 * CH:3 * CH + NB * P]
        wout_raw = big[:, 3 * CH + NB * P:3 * CH + 2 * NB * P]
        gelu = big[:, 3 * CH:3 * CH + T]
        xs = sb("xs", [P, T])
        scr = sb("scr", [P, 9216])
        x_rev = scr[:, 0:2048]
        w1_raw = scr[:, 2048:2560]
        w2_raw = scr[:, 2560:3072]
        ids = scr[:, 3072:4096].bitcast(I32)
        gws = scr[:, 4096:5120]
        mask = [scr[:, 5120 + 1024 * i:6144 + 1024 * i] for i in range(2)]
        gsum = scr[:, 7168:9216]
        gated = [scr[:, 512 * i:512 * i + 512] for i in range(RING)]
        hid = [scr[:, 2048 + 512 * i:2560 + 512 * i] for i in range(2)] + [scr[:, 7168:7680]]
        turn = [scr[:, 3072 + 512 * i:3584 + 512 * i] for i in range(2)] + [scr[:, 7680:8192]]
        whole = [scr[:, 4096 + 512 * i:4608 + 512 * i] for i in range(2)]
        o_sb = scr[:, 5120:5632]
        xn2 = scr[:, 5632:6144]
        y_sb = scr[:, 6144:6656]
        fin = scr[:, 6656:7168]
        xt_h, xt_l = sb("xt_h", [P, T], F32R), sb("xt_l", [P, T], F32R)
        win_h, win_l = sb("win_h", [P, NB * P], F32R), sb("win_l", [P, NB * P], F32R)
        wout_h, wout_l = sb("wout_h", [P, NB * P], F32R), sb("wout_l", [P, NB * P], F32R)
        w1_h, w1_l = sb("w1_h", [P, F], F32R), sb("w1_l", [P, F], F32R)
        w2_h, w2_l = sb("w2_h", [P, F], F32R), sb("w2_l", [P, F], F32R)
        hb_h, hb_l = sb("hb_h", [P, RING, GT], F32R), sb("hb_l", [P, RING, GT], F32R)
        x2_h, x2_l = sb("x2_h", [P, GT], F32R), sb("x2_l", [P, GT], F32R)
        act_h, act_l = sb("act_h", [P, 2, GT], F32R), sb("act_l", [P, 2, GT], F32R)
        ones = sb("ones", [P, P])
        ident = sb("ident", [P, P])
        flip = sb("flip", [P, P])
        pairs = sb("pairs", [P, 32])
        nhalf = sb("nhalf", [P, TG])
        kp = sb("kp", [P, 2 * L])
        NF = 4 * FB + 1
        ffn_rows = sb("ffn_rows", [NF, P])
        fc = sb("fc", [P, NF])
        s4 = sb("s4", [P, 4 * N + 2])
        ar, ai, cr, ci = (s4[:, N * i:N * i + N] for i in range(4))
        ldt, dsk = s4[:, 4 * N:4 * N + 1], s4[:, 4 * N + 1:4 * N + 2]
        NA = N + FB
        ang, kturn, rest, sn, sh, cs, tq = (sb(n, [P, NA]) for n in ("ang", "kturn", "rest", "sn", "sh", "cs", "tq"))
        dt_ = sb("dt_", [P, 1])
        ea, dre, mag, zm, are, den, inv, t0, t1, t2, t3, nr, ni = (
            sb(n, [P, N]) for n in ("ea", "dre", "mag", "zm", "are", "den", "inv", "t0", "t1", "t2", "t3", "nr", "ni"))
        qpow = sb("qpow", [P, 8 * 2 * N])
        ppow = sb("ppow", [P, 8 * 2 * N])
        zhi = sb("zhi", [P, 3 * 2 * N])
        td = sb("td", [P, 3 * 2 * N])
        te = sb("te", [P, 3 * 2 * N])
        tp = sb("tp", [P, 4 * 2 * N])
        tr = sb("tr", [P, 4 * 2 * N])
        cff, tbias = sb("cff", [P, FB]), sb("tbias", [P, FB])
        stat = sb("stat", [P, TG, 6])
        mv = sb("mv", [P, TG, 2])
        ve = sb("ve", [P, TG])
        rs = sb("rs", [P, TG])

        bank = ctx.enter_context(nc.psum_tensor("bank", [P, 8, 512], F32))
        conv_ps = bank[:, 0:4, :].rearrange("p a b -> p (a b)")
        o_ps, y_ps, t_ps = bank[:, 0, :], bank[:, 3, :], bank[:, 7, :]
        f_ps = [bank[:, 1, :], bank[:, 2, :]]
        h_ps = [bank[:, 4, :], bank[:, 5, :], bank[:, 6, :]]

        s_par, s_rows, s_x, s_gin, s_win, s_wout, s_w12 = (
            sem(n) for n in ("s_par", "s_rows", "s_x", "s_gin", "s_win", "s_wout", "s_w12"))
        s_cst, s_fc, s_fcc, s_exp, s_dre, s_mag, s_rest, s_sin, s_inv, s_zm, s_zhi, s_pp, s_red, s_kp, s_kpad = (
            sem(n) for n in ("s_cst", "s_fc", "s_fcc", "s_exp", "s_dre", "s_mag", "s_rest", "s_sin", "s_inv", "s_zm",
                             "s_zhi", "s_pp", "s_red", "s_kp", "s_kpad"))
        s_toep = [sem(f"s_toep{c}") for c in range(G)]
        s_zero, s_flip, s_xr, s_wt, s_whi, s_wlo, s_w12h, s_w12l = (
            sem(n) for n in ("s_zero", "s_flip", "s_xr", "s_wt", "s_whi", "s_wlo", "s_w12h", "s_w12l"))
        s_mask, s_gmm, s_gev, s_gd, s_conv, s_gelu, s_z1 = (
            sem(n) for n in ("s_mask", "s_gmm", "s_gev", "s_gd", "s_conv", "s_gelu", "s_z1"))
        s_gate = [sem(f"s_gate{g}") for g in range(G)]
        s_dchain, s_pchain = sem("s_dchain"), sem("s_pchain")
        s_var, s_rstd = sem("s_var"), sem("s_rstd")
        s_xn1, s_xt, s_xth, s_xtl = sem("s_xn1"), sem("s_xt"), sem("s_xth"), sem("s_xtl")
        s_in, s_gated, s_hi, s_lo, s_out = sem("s_in"), sem("s_gated"), sem("s_hi"), sem("s_lo"), sem("s_out")
        s_oev, s_ot, s_z2, s_xn2, s_x2t, s_x2h, s_x2l = (
            sem(n) for n in ("s_oev", "s_ot", "s_z2", "s_xn2", "s_x2t", "s_x2h", "s_x2l"))
        s_fin, s_fev, s_frac, s_sine, s_q, s_ah, s_al, s_fout = (
            sem(n) for n in ("s_fin", "s_fev", "s_frac", "s_sine", "s_q", "s_ah", "s_al", "s_fout"))
        s_yev, s_yt, s_z3, s_res, s_store = sem("s_yev"), sem("s_yt"), sem("s_z3"), sem("s_res"), sem("s_store")

        toks = "(c p) h -> p c h"
        x_v = x.rearrange("b l h -> (b l) h").rearrange(toks, p=P)
        out_v = out.rearrange("b l h -> (b l) h").rearrange(toks, p=P)
        gw_v = gate_w.rearrange("b k s -> (b k) s").rearrange("(c p) s -> p c s", p=P)
        id_v = gate_id.rearrange("b k s -> (b k) s").rearrange("(c p) s -> p c s", p=P)
        xs_c = xs[:, :].rearrange("p (c h) -> p c h", h=H)

        def grp(t, g):
            return t[:, g * GT:(g + 1) * GT]

        norms = [("a", 0)]
        for s in range(G + 1):
            if s + 1 < G:
                norms.append(("a", s + 1))
            if s >= 2:
                norms.append(("c", s - 2))
            if s >= 1:
                norms.append(("b", s - 1))
        norms.append(("c", G - 1))
        turn_of = {n: i for i, n in enumerate(norms)}

        block = ctx.enter_context(nc.Block())

        @block.sync
        def _(sp):
            sp.dma_start(ldt, log_dt.rearrange("(h a) -> h a", a=1)).then_inc(s_par, 16)
            for dst, src in ((ar, a_real), (ai, a_imag), (cr, c_real), (ci, c_imag)):
                sp.dma_start(dst, src).then_inc(s_par, 16)
            sp.dma_start(dsk, bass.AP(d_skip.tensor, 0, [[0, P], [1, 1]])).then_inc(s_par, 16)
            sp.dma_start(xs_c, x_v).then_inc(s_x, 16)
            sp.dma_start(w1_raw, w1).then_inc(s_w12, 16)
            sp.dma_start(w2_raw.rearrange("p (c d) -> p c d", d=P), w2.rearrange("(c p) d -> p c d", p=P)) \
                .then_inc(s_w12, 16)
            sp.wait_ge(s_kp, 1)
            sp.dma_start(kpad, kp[:, :]).then_inc(s_kpad, 16)
            sp.wait_ge(s_kpad, 16)
            for c in range(G):
                if c == 0:
                    sp.wait_ge(s_red, 1)
                if c == 3:
                    sp.wait_ge(s_wt, 8)
                for q in range(PAIR):
                    sp.dma_start(toep[L * q:L * q + L, HC * c:HC * c + HC, L * q:L * q + L],
                                 bass.AP(kpad.tensor, 1 + c * HC * 2 * L, [[1, L], [2 * L, HC], [1, L]])) \
                        .then_inc(s_toep[c], 16)
            sp.wait_ge(s_gev, 2)
            for j in range(4):
                for a in range(2):
                    sp.dma_start(bass.AP(gates.tensor, (j + 4 * a) * T, [[L, PAIR], [P, C], [1, L]]),
                                 gsum[32 * j:32 * j + PAIR, a * C * L:(a + 1) * C * L]
                                 .rearrange("q (c s) -> q c s", s=L)).then_inc(s_gd, 16)
            sp.wait_ge(s_gd, 16 * E)
            for g in range(G):
                sp.wait_ge(s_conv, g + 1)
                if g == 3:
                    sp.wait_ge(s_z1, G)
                sp.dma_start(big[:, g * CH:(g + 1) * CH].rearrange("p (e t) -> p e t", e=E),
                             bass.AP(gates.tensor, g * GT, [[0, P], [T, E], [1, GT]])).then_inc(s_gate[g], 16)
            for g in range(G):
                sp.wait_ge(s_res, g + 1)
                sp.dma_start(out_v[:, g * TG:(g + 1) * TG, :], fin.rearrange("p (c h) -> p c h", h=H)) \
                    .then_inc(s_store, 16)
            sp.wait_ge(s_store, 16 * G)

        @block.gpsimd
        def _(pool):
            chain = [0]

            def link(ins):
                chain[0] += 1
                ins.then_inc(s_pchain, 1)
                pool.wait_ge(s_pchain, chain[0])

            nc.gpsimd.memset(pairs[:, :], 0.0).then_inc(s_cst, 1)
            nc.gpsimd.memset(nhalf[:, :], -0.5).then_inc(s_cst, 1)
            link(nc.gpsimd.memset(ones[:, :], 1.0))
            pool.wait_ge(s_cst, 2)
            nc.gpsimd.affine_select(out=ident[:, :], in_=ones[:, :], compare_op=ALU.is_equal, fill=0.0,
                                    base=0, pattern=[[-1, P]], channel_multiplier=1).then_inc(s_cst, 1)
            for q in range(PAIR):
                nc.gpsimd.affine_select(out=flip[:, L * q:L * q + L], in_=ones[:, 0:L], compare_op=ALU.is_equal,
                                        fill=0.0, base=1 - L - 2 * L * q + L * q, pattern=[[1, L]],
                                        channel_multiplier=1).then_inc(s_cst, 1)
            pool.wait_ge(s_cst, 5)
            for q in range(PAIR):
                nc.gpsimd.memset(pairs[L * q:L * q + L, q:q + 1], 1.0).then_inc(s_cst, 1)
                pool.wait_ge(s_cst, 6 + q)
            zeros = [0]

            def zero_blocks(c):
                for q in range(PAIR):
                    nc.gpsimd.memset(toep[L * q:L * q + L, HC * c:HC * c + HC, L * (1 - q):L * (1 - q) + L], 0.0) \
                        .then_inc(s_zero, 1)
                    zeros[0] += 1
                    pool.wait_ge(s_zero, zeros[0])

            zero_blocks(1)
            zero_blocks(2)

            pool.wait_ge(s_par, 96)
            pool.wait_ge(s_exp, 1)
            tt = nc.gpsimd.tensor_tensor
            nc.gpsimd.tensor_scalar(are[:, :], ea[:, :], -1.0, None, ALU.mult)
            tt(t0[:, :], ea[:, :], ea[:, :], ALU.mult)
            link(tt(t1[:, :], ai, ai, ALU.mult))
            link(tt(den[:, :], t0[:, :], t1[:, :], ALU.add))
            nc.gpsimd.tensor_scalar(den[:, :], den[:, :], 0.5, None, ALU.mult).then_inc(s_pp, 1)
            pool.wait_ge(s_zm, 1)
            zc = qpow[:, 3 * N:4 * N]
            tt(t0[:, :], cr, zm[:, :], ALU.mult)
            tt(t1[:, :], ci, zc, ALU.mult)
            tt(t2[:, :], ci, zm[:, :], ALU.mult)
            link(tt(t3[:, :], cr, zc, ALU.mult))
            tt(nr[:, :], t0[:, :], t1[:, :], ALU.add)
            link(tt(ni[:, :], t2[:, :], t3[:, :], ALU.subtract))
            tt(t0[:, :], nr[:, :], are[:, :], ALU.mult)
            tt(t1[:, :], ni[:, :], ai, ALU.mult)
            tt(t2[:, :], ni[:, :], are[:, :], ALU.mult)
            link(tt(t3[:, :], nr[:, :], ai, ALU.mult))
            tt(nr[:, :], t0[:, :], t1[:, :], ALU.add)
            link(tt(ni[:, :], t2[:, :], t3[:, :], ALU.subtract))
            pool.wait_ge(s_inv, 1)
            tt(ppow[:, 0:N], nr[:, :], inv[:, :], ALU.mult)
            link(tt(ppow[:, N:2 * N], ni[:, :], inv[:, :], ALU.mult))
            for i, m in enumerate((1, 2, 4)):
                pool.wait_ge(s_zhi, i + 1)
                src = ppow[:, 0:2 * N * m]
                yr = zhi[:, 2 * N * i:2 * N * i + N]
                yc = zhi[:, 2 * N * i + N:2 * N * i + 2 * N]
                tt(view(tp[:, :], [[2 * N, m], [N, 2], [1, N]]), view(src, [[2 * N, m], [N, 2], [1, N]]),
                   view(yr, [[0, m], [0, 2], [1, N]]), ALU.mult)
                link(tt(view(tr[:, :], [[2 * N, m], [N, 2], [1, N]]), view(src, [[2 * N, m], [N, 2], [1, N]]),
                        view(yc, [[0, m], [0, 2], [1, N]]), ALU.mult))
                dst = ppow[:, 2 * N * m:4 * N * m]
                tt(view(dst, [[2 * N, m], [1, N]]), view(tp[:, :], [[2 * N, m], [1, N]]),
                   view(tr[:, :], [[2 * N, m], [1, N]], N), ALU.add)
                last = tt(view(dst, [[2 * N, m], [1, N]], N), view(tp[:, :], [[2 * N, m], [1, N]], N),
                          view(tr[:, :], [[2 * N, m], [1, N]]), ALU.subtract)
                if i < 2:
                    link(last)
                else:
                    last.then_inc(s_pp, 1)

            pool.wait_ge(s_pp, 2)
            pool.wait_ge(s_w12h, 2)
            tt(w1_l[:, :], w1_raw, w1_h[:, :].bitcast(F32), ALU.subtract).then_inc(s_w12l, 1)
            tt(w2_l[:, :], w2_raw, w2_h[:, :].bitcast(F32), ALU.subtract).then_inc(s_w12l, 1)
            pool.wait_ge(s_w12l, 2)
            for c in (0, 3):
                if c == 0:
                    pool.wait_ge(s_red, 1)
                else:
                    pool.wait_ge(s_wt, 8)
                zero_blocks(c)

            def add_gelu(g):
                pool.wait_ge(s_gelu, g + 1)
                tt(grp(xs, g), grp(xs, g), grp(gelu, g), ALU.add).then_inc(s_z1, 1)

            def inv_std(kind, g):
                t = turn_of[kind, g]
                pool.wait_ge(s_var, t + 1)
                tt(rs[:, :], ve[:, :], nhalf[:, :], ALU.pow).then_inc(s_rstd, 1)

            def low(n):
                pool.wait_ge(s_hi, n + 1)
                if n >= RING:
                    pool.wait_ge(s_out, n - RING + 1)
                tt(hb_l[:, n % RING, :], gated[n % RING], hb_h[:, n % RING, :].bitcast(F32), ALU.subtract) \
                    .then_inc(s_lo, 1)

            add_gelu(0)
            inv_std("a", 0)
            for s in range(G + 1):
                if s == 0:
                    add_gelu(1)
                for j in range(NB):
                    if j == 1 and s + 1 < G:
                        inv_std("a", s + 1)
                    if j == 3 and s >= 2:
                        inv_std("c", s - 2)
                    if j == 6 and s >= 1:
                        inv_std("b", s - 1)
                    if j == 12 and s + 2 < G:
                        add_gelu(s + 2)
                    if s < G:
                        low(NB * s + j)
            inv_std("c", G - 1)

        @block.scalar
        def _(act):
            act.dma_start(ffn_rows[0:FB, :], theta.rearrange("(c p) -> c p", p=P)).then_inc(s_rows, 16)
            for i, v in enumerate((q_real, q_imag, b1)):
                act.dma_start(ffn_rows[FB * (i + 1):FB * (i + 2), :], v.rearrange("(c p) -> c p", p=P)) \
                    .then_inc(s_rows, 16)
            act.dma_start(ffn_rows[4 * FB:NF, :], b2.rearrange("(c p) -> c p", p=P)).then_inc(s_rows, 16)
            act.dma_start(ids.rearrange("p (c s) -> p c s", s=L), id_v).then_inc(s_gin, 16)
            act.dma_start(gws.rearrange("p (c s) -> p c s", s=L), gw_v).then_inc(s_gin, 16)
            act.dma_start(win_raw.rearrange("p (k i) -> p k i", i=P), w_in.rearrange("e (c d) i -> d (e c) i", d=P)) \
                .then_inc(s_win, 16)
            act.dma_start(wout_raw.rearrange("p (e d) -> p e d", d=D), w_out.rearrange("e i d -> i e d")) \
                .then_inc(s_wout, 16)
            av = nc.scalar.activation
            act.wait_ge(s_par, 96)
            av(dt_[:, :], ldt, ACT.Exp)
            av(ea[:, :], ar, ACT.Exp).then_inc(s_exp, 1)
            act.wait_ge(s_dre, 1)
            av(mag[:, :], dre[:, :], ACT.Exp).then_inc(s_mag, 1)
            act.wait_ge(s_rest, 1)
            av(sn[:, :], rest[:, :], ACT.Sin)
            av(sh[:, :], rest[:, :], ACT.Sin, scale=0.5).then_inc(s_sin, 1)
            for i in range(G):
                act.wait_ge(s_flip, i + 1)
                av(grp(x_rev, i), bank[:, i, :], ACT.Copy).then_inc(s_xr, 1)
            act.wait_ge(s_w12, 32)
            av(w1_h[:, :], w1_raw, ACT.Copy).then_inc(s_w12h, 1)
            av(w2_h[:, :], w2_raw, ACT.Copy).then_inc(s_w12h, 1)
            for k in range(8):
                act.wait_ge(s_wt, k + 1)
                dst = (win_h if k < 4 else wout_h)[:, (k % 4) * 512:(k % 4) * 512 + 512]
                av(dst, bank[:, k % 4, :], ACT.Copy).then_inc(s_whi, 1)
                if k == 7:
                    act.wait_ge(s_gmm, 8)
                    av(gsum[:, 0:1024], bank[:, 4:6, :].rearrange("p a b -> p (a b)"), ACT.Copy).then_inc(s_gev, 1)
            act.wait_ge(s_gmm, 16)
            av(gsum[:, 1024:2048], bank[:, 6:8, :].rearrange("p a b -> p (a b)"), ACT.Copy).then_inc(s_gev, 1)

            def gelu_of(g):
                av(view(grp(gelu, g), [[P, TG], [1, P]]), view(conv_ps, [[1, TG], [C, H]], g * TG), ACT.Gelu) \
                    .then_inc(s_gelu, 1)

            def xt_high(g):
                act.wait_ge(s_xt, g + 1)
                av(grp(xt_h, g), t_ps, ACT.Copy).then_inc(s_xth, 1)

            act.wait_ge(s_conv, G)
            for g in range(G):
                gelu_of(g)
            xt_high(0)

            def high(n):
                act.wait_ge(s_gated, n + 1)
                if n >= RING:
                    act.wait_ge(s_out, n - RING + 1)
                av(hb_h[:, n % RING, :], gated[n % RING], ACT.Copy).then_inc(s_hi, 1)

            def ffn_parts(m):
                f = m % FB
                act.wait_ge(s_fin, m + 1)
                if m >= 3:
                    act.wait_ge(s_al, m - 2)
                av(hid[m % 3], f_ps[m % 2], ACT.Identity, bias=fc[:, 3 * FB + f:3 * FB + f + 1])
                av(turn[m % 3], f_ps[m % 2], ACT.Identity, bias=tbias[:, f:f + 1], scale=0.1 * INV_TWO_PI) \
                    .then_inc(s_fev, 1)

            def ffn_sine(m):
                act.wait_ge(s_frac, m + 1)
                av(turn[m % 3], turn[m % 3], ACT.Sin, scale=TWO_PI_BELOW).then_inc(s_sine, 1)

            def ffn_high(m):
                act.wait_ge(s_q, m + 1)
                if m >= 2:
                    act.wait_ge(s_fout, m - 1)
                av(act_h[:, m % 2, :], hid[m % 3], ACT.Relu).then_inc(s_ah, 1)

            for s in range(G + 1):
                for j in range(NB):
                    if s < G:
                        high(NB * s + j)
                    if j == 0 and s >= 2:
                        act.wait_ge(s_fout, FB * (s - 1))
                        if s >= 3:
                            act.wait_ge(s_yt, s - 2)
                        av(y_sb, y_ps, ACT.Identity, bias=fc[:, 4 * FB:NF]).then_inc(s_yev, 1)
                    if j == 2 and s >= 1:
                        act.wait_ge(s_out, NB * s)
                        if s >= 2:
                            act.wait_ge(s_ot, s - 1)
                        av(o_sb, o_ps, ACT.Copy).then_inc(s_oev, 1)
                    if j == 3 and s + 1 < G:
                        xt_high(s + 1)
                    if j == 7 and s >= 1:
                        act.wait_ge(s_x2t, s)
                        if s >= 2:
                            act.wait_ge(s_fin, FB * (s - 1))
                        av(x2_h[:, :], t_ps, ACT.Copy).then_inc(s_x2h, 1)
                    if s >= 1:
                        m = FB * (s - 1) + j - 8
                        if 8 <= j < 12:
                            ffn_parts(m)
                        if 9 <= j < 13:
                            ffn_sine(m - 1)
                        if 10 <= j < 14:
                            ffn_high(m - 2)
            act.wait_ge(s_fout, FB * G)
            act.wait_ge(s_yt, G - 1)
            av(y_sb, y_ps, ACT.Identity, bias=fc[:, 4 * FB:NF]).then_inc(s_yev, 1)

        @block.vector
        def _(dve):
            chain = [0]

            def link(ins):
                chain[0] += 1
                ins.then_inc(s_dchain, 1)
                dve.wait_ge(s_dchain, chain[0])

            tt, ts, stt = nc.vector.tensor_tensor, nc.vector.tensor_scalar, nc.vector.scalar_tensor_tensor
            nc.vector.memset(kp[:, 0:L], 0.0)
            nc.vector.memset(qpow[:, 0:N], 1.0)
            link(nc.vector.memset(qpow[:, N:2 * N], 0.0))
            dve.wait_ge(s_par, 96)
            dve.wait_ge(s_exp, 1)
            ts(dre[:, :], ea[:, :], dt_[:, 0:1], -1.0, ALU.mult, ALU.mult).then_inc(s_dre, 1)
            ts(ang[:, 0:N], ai, dt_[:, 0:1], None, ALU.mult)
            dve.wait_ge(s_fc, 1)
            nc.vector.tensor_copy(fc[:, :], bank[:, 7, 0:NF]).then_inc(s_fcc, 1)
            link(nc.vector.tensor_copy(ang[:, N:NA], bank[:, 7, 0:FB]))
            link(ts(kturn[:, :], ang[:, :], INV_TWO_PI, ROUND, ALU.mult, ALU.add))
            link(ts(kturn[:, :], kturn[:, :], ROUND, None, ALU.subtract))
            link(stt(rest[:, :], kturn[:, :], -TWO_PI_HI, ang[:, :], ALU.mult, ALU.add))
            link(stt(rest[:, :], kturn[:, :], -TWO_PI_LO, rest[:, :], ALU.mult, ALU.add))
            ts(rest[:, :], rest[:, :], PI_BELOW, -PI_BELOW, ALU.min, ALU.max).then_inc(s_rest, 1)
            dve.wait_ge(s_sin, 1)
            link(tt(cs[:, :], sh[:, :], sh[:, :], ALU.mult))
            link(ts(cs[:, :], cs[:, :], -2.0, 1.0, ALU.mult, ALU.add))
            dve.wait_ge(s_mag, 1)
            z1 = qpow[:, 2 * N:4 * N]
            tt(z1[:, 0:N], mag[:, :], cs[:, 0:N], ALU.mult)
            link(stt(z1[:, N:2 * N], mag[:, :], -1.0, sn[:, 0:N], ALU.mult, ALU.mult))
            ts(zm[:, :], z1[:, 0:N], -1.0, None, ALU.add).then_inc(s_zm, 1)

            def square(dst, src):
                tt(td[:, 0:2 * N], src, src, ALU.mult)
                link(stt(dst[:, N:2 * N], src[:, 0:N], 2.0, src[:, N:2 * N], ALU.mult, ALU.mult))
                return tt(dst[:, 0:N], td[:, 0:N], td[:, N:2 * N], ALU.subtract)

            def times(dst, src, by, m):
                s3 = [[2 * N, m], [N, 2], [1, N]]
                tt(view(td[:, :], s3), view(src, s3), view(by[:, 0:N], [[0, m], [0, 2], [1, N]]), ALU.mult)
                link(tt(view(te[:, :], s3), view(src, s3), view(by[:, N:2 * N], [[0, m], [0, 2], [1, N]]), ALU.mult))
                s2 = [[2 * N, m], [1, N]]
                tt(view(dst, s2), view(td[:, :], s2), view(te[:, :], s2, N), ALU.subtract)
                return tt(view(dst, s2, N), view(td[:, :], s2, N), view(te[:, :], s2), ALU.add)

            def q_(c, m=1):
                return qpow[:, 2 * N * c:2 * N * (c + m)]

            link(square(q_(2), q_(1)))
            link(square(q_(4), q_(2)))
            square(zhi[:, 0:2 * N], q_(4)).then_inc(s_zhi, 1)
            dve.wait_ge(s_zhi, 1)
            square(zhi[:, 2 * N:4 * N], zhi[:, 0:2 * N]).then_inc(s_zhi, 1)
            dve.wait_ge(s_zhi, 2)
            square(zhi[:, 4 * N:6 * N], zhi[:, 2 * N:4 * N]).then_inc(s_zhi, 1)
            dve.wait_ge(s_zhi, 3)
            dve.wait_ge(s_pp, 1)
            nc.vector.reciprocal(inv[:, :], den[:, :]).then_inc(s_inv, 1)
            link(times(q_(3), q_(2), q_(1), 1))
            link(times(q_(5, 3), q_(1, 3), q_(4), 3))
            tt(tq[:, 0:FB], cs[:, N:NA], fc[:, FB:2 * FB], ALU.mult)
            link(tt(kturn[:, 0:FB], sn[:, N:NA], fc[:, 2 * FB:3 * FB], ALU.mult))
            link(tt(tq[:, 0:FB], tq[:, 0:FB], kturn[:, 0:FB], ALU.add))
            stt(cff[:, :], tq[:, 0:FB], 0.1, fc[:, 2 * FB:3 * FB], ALU.mult, ALU.mult)
            link(ts(tbias[:, :], rest[:, N:NA], INV_TWO_PI, None, ALU.mult))
            link(stt(tbias[:, :], fc[:, 3 * FB:4 * FB], 0.1 * INV_TWO_PI, tbias[:, :], ALU.mult, ALU.add))
            dve.wait_ge(s_pp, 2)
            half = 4 * 8 * 2 * N
            for i in range(2):
                o = view(prod[:, i * half:(i + 1) * half], [[16 * N, 4], [2 * N, 8], [1, 2 * N]])
                link(tt(o, view(ppow[:, :], [[2 * N, 4], [0, 8], [1, 2 * N]], 8 * N * i),
                        view(qpow[:, :], [[0, 4], [2 * N, 8], [1, 2 * N]]), ALU.mult))
            for i in range(2):
                last = nc.vector.tensor_reduce(
                    kp[:, L + 32 * i:L + 32 * i + 32],
                    prod[:, i * half:(i + 1) * half].rearrange("p (l n) -> p l n", n=2 * N), AX_X, ALU.add)
            last.then_inc(s_red, 1)
            dve.wait_ge(s_red, 1)
            ts(kp[:, L:L + 1], kp[:, L:L + 1], dsk, None, ALU.add).then_inc(s_kp, 1)

            dve.wait_ge(s_gin, 32)
            for e in range(E):
                if e >= 2:
                    dve.wait_ge(s_gmm, 2 * (e - 1))
                stt(mask[e % 2], ids, float(e), gws, ALU.is_equal, ALU.mult).then_inc(s_mask, 1)
                dve.wait_ge(s_whi, e + 1)
                hi = (win_h if e < 4 else wout_h)[:, (e % 4) * 512:(e % 4) * 512 + 512]
                lo = (win_l if e < 4 else wout_l)[:, (e % 4) * 512:(e % 4) * 512 + 512]
                tt(lo, bank[:, e % 4, :], hi.bitcast(F32), ALU.subtract).then_inc(s_wlo, 1)

            def spread(src, kind, g):
                for c in range(TG):
                    last = nc.vector.bn_stats(stat[:, c, :], src[:, c * P:(c + 1) * P])
                link(last)
                for c in range(TG):
                    last = nc.vector.bn_aggr(mv[:, c, :], stat[:, c, :])
                link(last)
                ts(ve[:, :], view(mv[:, 0, :], [[2, TG]], 1), EPS, None, ALU.add).then_inc(s_var, 1)

            def normalise(dst, src, kind, g, done):
                dve.wait_ge(s_rstd, turn_of[kind, g] + 1)
                for c in range(TG):
                    last = ts(dst[:, c * P:(c + 1) * P], src[:, c * P:(c + 1) * P], mv[:, c, 0:1], rs[:, c:c + 1],
                              ALU.subtract, ALU.mult)
                last.then_inc(done, 1)

            def spread_a(g):
                dve.wait_ge(s_z1, g + 1)
                spread(grp(xs, g), "a", g)

            def xt_low(g):
                dve.wait_ge(s_xth, g + 1)
                tt(grp(xt_l, g), t_ps, grp(xt_h, g).bitcast(F32), ALU.subtract).then_inc(s_xtl, 1)

            spread_a(0)
            normalise(grp(xs, 0), grp(xs, 0), "a", 0, s_xn1)
            xt_low(0)

            def gate_block(n):
                g, j = divmod(n, NB)
                if j == 0:
                    dve.wait_ge(s_gate[g], 16)
                dve.wait_ge(s_in, n + 1)
                if n >= RING:
                    dve.wait_ge(s_hi, n - RING + 1)
                    dve.wait_ge(s_lo, n - RING + 1)
                e = j // DH
                stt(gated[n % RING], h_ps[n % 3], 0.0, big[:, g * CH + e * GT:g * CH + (e + 1) * GT],
                    ALU.max, ALU.mult).then_inc(s_gated, 1)

            def ffn_frac(m):
                dve.wait_ge(s_fev, m + 1)
                link(ts(whole[m % 2], turn[m % 3], ROUND, ROUND, ALU.add, ALU.subtract))
                tt(turn[m % 3], turn[m % 3], whole[m % 2], ALU.subtract).then_inc(s_frac, 1)

            def ffn_q(m):
                dve.wait_ge(s_sine, m + 1)
                stt(hid[m % 3], turn[m % 3], cff[:, m % FB:m % FB + 1], hid[m % 3], ALU.mult, ALU.add) \
                    .then_inc(s_q, 1)

            def ffn_low(m):
                dve.wait_ge(s_ah, m + 1)
                if m >= 2:
                    dve.wait_ge(s_fout, m - 1)
                stt(act_l[:, m % 2, :], hid[m % 3], 0.0, act_h[:, m % 2, :].bitcast(F32), ALU.max, ALU.subtract) \
                    .then_inc(s_al, 1)

            def last_norm_a(g):
                dve.wait_ge(s_yt, g + 1)
                if g >= 1:
                    dve.wait_ge(s_store, 16 * g)
                tt(fin, t_ps, xn2, ALU.add).then_inc(s_z3, 1)
                dve.wait_ge(s_z3, g + 1)
                spread(fin, "c", g)

            for s in range(G + 1):
                for j in range(NB):
                    if s < G:
                        gate_block(NB * s + j)
                    if s + 1 < G:
                        if j == 0:
                            spread_a(s + 1)
                        if j == 1:
                            normalise(grp(xs, s + 1), grp(xs, s + 1), "a", s + 1, s_xn1)
                        if j == 4:
                            xt_low(s + 1)
                    if s >= 2:
                        if j == 2:
                            last_norm_a(s - 2)
                        if j == 3:
                            normalise(fin, fin, "c", s - 2, s_res)
                    if s >= 1:
                        if j == 5:
                            dve.wait_ge(s_ot, s)
                            tt(xn2, t_ps, grp(xs, s - 1), ALU.add).then_inc(s_z2, 1)
                            dve.wait_ge(s_z2, s)
                            spread(xn2, "b", s - 1)
                        if j == 6:
                            normalise(xn2, xn2, "b", s - 1, s_xn2)
                        if j == 8:
                            dve.wait_ge(s_x2h, s)
                            if s >= 2:
                                dve.wait_ge(s_fin, FB * (s - 1))
                            tt(x2_l[:, :], t_ps, x2_h[:, :].bitcast(F32), ALU.subtract).then_inc(s_x2l, 1)
                        m = FB * (s - 1) + j - 8
                        if 8 <= j < 12:
                            ffn_frac(m)
                        if 9 <= j < 13:
                            ffn_q(m - 1)
                        if 10 <= j < 14:
                            ffn_low(m - 2)
            last_norm_a(G - 1)
            normalise(fin, fin, "c", G - 1, s_res)

        @block.tensor
        def _(pe):
            mm = nc.tensor.matmul
            pe.wait_ge(s_cst, 7)
            pe.wait_ge(s_rows, 80)
            nc.tensor.transpose(bank[:, 7, 0:NF], ffn_rows[:, :], ident[0:NF, 0:NF]).then_inc(s_fc, 1)
            pe.wait_ge(s_x, 16)
            for i in range(G):
                mm(bank[:, i, :], flip[:, :], grp(xs, i), start=True, stop=True).then_inc(s_flip, 1)

            def turn_weights(k):
                if k < 4:
                    pe.wait_ge(s_xr, k + 1)
                else:
                    pe.wait_ge(s_wlo, k - 3)
                pe.wait_ge(s_win if k < 4 else s_wout, 16)
                raw = win_raw if k < 4 else wout_raw
                for i in range(4):
                    o = (k % 4) * 512 + i * P
                    last = nc.tensor.transpose(bank[:, k % 4, i * P:(i + 1) * P], raw[:, o:o + P], ident[:, :])
                last.then_inc(s_wt, 1)

            for k in range(4):
                turn_weights(k)
            pe.wait_ge(s_fcc, 1)
            for e in range(E):
                pe.wait_ge(s_mask, e + 1)
                for i in range(2):
                    mm(bank[32 * (e % 4):32 * (e % 4) + 32, 4 + 2 * (e // 4) + i, :], pairs[:, :],
                       mask[e % 2][:, i * 512:(i + 1) * 512], start=True, stop=True).then_inc(s_gmm, 1)
                if e < 4:
                    turn_weights(e + 4)
            pe.wait_ge(s_wlo, 8)
            pe.wait_ge(s_zero, 8)
            xr = x_rev.rearrange("p (c h) -> p h c", h=H)
            for c in range(G):
                pe.wait_ge(s_toep[c], 32)
                for h in range(HC * c, HC * c + HC):
                    last = mm(conv_ps[:, h * C:(h + 1) * C], toep[:, h, :], xr[:, h, :], start=True, stop=True)
                last.then_inc(s_conv, 1)

            def three(dst, wh, wl, vh, vl, first, last):
                mm(dst, wh, vh, start=first, stop=False)
                mm(dst, wl, vh, start=False, stop=False)
                return mm(dst, wh, vl, start=False, stop=last)

            def xt_turn(g):
                pe.wait_ge(s_xn1, g + 1)
                for c in range(TG):
                    o = g * GT + c * P
                    last = nc.tensor.transpose(t_ps[:, c * P:(c + 1) * P], xs[:, o:o + P], ident[:, :])
                last.then_inc(s_xt, 1)

            def turn4(src, done):
                for c in range(TG):
                    last = nc.tensor.transpose(t_ps[:, c * P:(c + 1) * P], src[:, c * P:(c + 1) * P], ident[:, :])
                last.then_inc(done, 1)

            pe.wait_ge(s_gev, 2)
            xt_turn(0)
            pe.wait_ge(s_w12l, 2)

            def first_product(n):
                g, j = divmod(n, NB)
                if j == 0:
                    pe.wait_ge(s_xtl, g + 1)
                if n >= 3:
                    pe.wait_ge(s_gated, n - 2)
                w = slice(j * P, (j + 1) * P)
                three(h_ps[n % 3], win_h[:, w], win_l[:, w], grp(xt_h, g), grp(xt_l, g), True, True) \
                    .then_inc(s_in, 1)

            def second_product(n):
                g, j = divmod(n, NB)
                if n == 0:
                    pe.wait_ge(s_gelu, G)
                if j == 0 and g >= 1:
                    pe.wait_ge(s_oev, g)
                pe.wait_ge(s_lo, n + 1)
                w = slice(j * P, (j + 1) * P)
                r = n % RING
                three(o_ps, wout_h[:, w], wout_l[:, w], hb_h[:, r, :], hb_l[:, r, :], j == 0, j == NB - 1) \
                    .then_inc(s_out, 1)

            def ffn_first(m):
                f = m % FB
                if f == 0:
                    pe.wait_ge(s_x2l, m // FB + 1)
                if m >= 2:
                    pe.wait_ge(s_fev, m - 1)
                w = slice(f * P, (f + 1) * P)
                three(f_ps[m % 2], w1_h[:, w], w1_l[:, w], x2_h[:, :], x2_l[:, :], True, True).then_inc(s_fin, 1)

            def ffn_second(m):
                f = m % FB
                if f == 0 and m >= FB:
                    pe.wait_ge(s_yev, m // FB)
                pe.wait_ge(s_al, m + 1)
                w = slice(f * P, (f + 1) * P)
                three(y_ps, w2_h[:, w], w2_l[:, w], act_h[:, m % 2, :], act_l[:, m % 2, :], f == 0, f == FB - 1) \
                    .then_inc(s_fout, 1)

            for s in range(G + 1):
                for j in range(NB):
                    n = NB * s + j
                    if s < G:
                        first_product(n)
                    if n >= LAG and n - LAG < NB * G:
                        second_product(n - LAG)
                    if j == 1 and s >= 2:
                        pe.wait_ge(s_yev, s - 1)
                        turn4(y_sb, s_yt)
                    if j == 3 and s + 1 < G:
                        if s >= 2:
                            pe.wait_ge(s_z3, s - 1)
                        xt_turn(s + 1)
                    if s >= 1:
                        if j == 5:
                            pe.wait_ge(s_oev, s)
                            if s + 1 < G:
                                pe.wait_ge(s_xtl, s + 2)
                            elif s >= 2:
                                pe.wait_ge(s_z3, s - 1)
                            turn4(o_sb, s_ot)
                        if j == 7:
                            pe.wait_ge(s_xn2, s)
                            turn4(xn2, s_x2t)
                        m = FB * (s - 1) + j - 8
                        if 8 <= j < 12:
                            ffn_first(m)
                        if 11 <= j < 15:
                            ffn_second(m - 3)
            pe.wait_ge(s_yev, G)
            turn4(y_sb, s_yt)


_INS = ['x', 'ctx_512', 'itok_BxS2xS_0_7', 'L0_attn_log_dt', 'L0_attn_A_real', 'L0_attn_A_imag', 'L0_attn_C_real',
        'L0_attn_C_imag', 'L0_attn_D', 'L0_xattn_proj_in', 'L0_xattn_proj_out', 'L0_ffn_W1', 'L0_ffn_b1',
        'L0_ffn_quantum_phases', 'L0_ffn_quantum_weights_real', 'L0_ffn_quantum_weights_imag', 'L0_ffn_W2',
        'L0_ffn_b2']


def kernel(**inputs):
    import numpy as _np
    import concourse.bacc as _bacc
    from concourse import mybir as _mybir
    from concourse.bass_utils import run_bass_kernel_spmd as _run

    nc = _bacc.Bacc("TRN2", target_bir_lowering=False, num_devices=1)
    arrays, args = {}, []
    for name in _INS:
        a = _np.ascontiguousarray(inputs[name])
        if a.ndim == 0:
            a = a.reshape(1)
        arrays[f"in_{name}_dram"] = a
        args.append(nc.dram_tensor(f"in_{name}_dram", a.shape, _mybir.dt.from_np(a.dtype), kind="ExternalInput").ap())
    fp32 = _mybir.dt.float32
    b, l, h = inputs['x'].shape
    experts = inputs['L0_xattn_proj_in'].shape[0]
    args.append(nc.dram_tensor("kpad", (h, 2 * l), fp32, kind="Internal").ap())
    args.append(nc.dram_tensor("gates", (experts, b * l), fp32, kind="Internal").ap())
    args.append(nc.dram_tensor("out_0_dram", (b, l, h), fp32, kind="ExternalOutput").ap())
    s4d_moe_ffn_decoder(nc, *args)
    r = _run(nc, [arrays], core_ids=[0])
    return r.results[0]["out_0_dram"]
```

```python
from contextlib import ExitStack

import concourse.bass as bass
from concourse import mybir

F32 = mybir.dt.float32
F32R = mybir.dt.float32r
I32 = mybir.dt.int32
ALU = mybir.AluOpType
ACT = mybir.ActivationFunctionType
AX_X = mybir.AxisListType.X

P = 128
TWO_PI_HI = 6.28125
TWO_PI_LO = 0.0019353071795864769
INV_TWO_PI = 0.15915494309189535
ROUND = 12582912.0
PI_BELOW = 3.1415925
TWO_PI_BELOW = 6.283185
EPS = 1e-5


def view(ap, dims, shift=0):
    return bass.AP(ap.tensor, ap.offset + shift, [list(ap.ap[0])] + [list(d) for d in dims])


SLOTS = {
    "y_turn": -12, "z1": -11, "rstd1": -10, "norm1": -8, "xt_turn": -5, "xt_high": -4, "xt_low": -3,
    "o_evac": 18, "o_turn": 22, "z2": 23, "rstd2": 24, "norm2": 25, "x2_turn": 26, "x2_high": 27, "x2_low": 28,
    "f_first": 29, "f_parts": 30, "f_frac": 31, "f_sine": 32, "f_mix": 33, "f_high": 34, "f_low": 35,
    "f_second": 36,
    "y_evac": 40, "out_turn": 41, "z3": 42, "rstd3": 43, "norm3": 44,
}
PER_BLOCK = {"f_first", "f_parts", "f_frac", "f_sine", "f_mix", "f_high", "f_low", "f_second"}


def s4d_moe_ffn_decoder(nc, x, x_rev, gate_w, gate_id, s4d_par, w_in, w_out, w1, w2, ffn_par,
                        kpad, gates, y_dram, out):
    T = x.shape[1]
    L = gate_w.shape[0] // 2
    H = x.shape[0]
    N = (s4d_par.shape[1] - 2) // 4
    B = T // L
    E, F = gates.shape[0], w1.shape[1]
    NB = w_in.shape[1] // P
    DH = NB // E
    GT = 512
    G = T // GT
    TG = GT // P
    BG = GT // L
    FB = F // P
    LAG = 3
    RING = 4
    JC = 4
    HH = H // 2 // JC
    HQ = H // 4
    assert H == P and L == 64 and B == 32 and FB == 4 and NB == 16 and G == 4 and N == 32 and E == 8

    with ExitStack() as ctx:
        def sb(name, shape, dt=F32):
            return ctx.enter_context(nc.sbuf_tensor(name, shape, dt))

        def sem(name):
            return ctx.enter_context(nc.semaphore(name))

        GS = E * GT
        NGB = 3
        gbuf = sb("gbuf", [P, NGB * GS])
        gate_g = [gbuf[:, i * GS:(i + 1) * GS] for i in range(NGB)]
        prod = gate_g[0]
        win_raw, wout_raw = gate_g[1][:, 0:NB * P], gate_g[1][:, NB * P:2 * NB * P]
        ids = gate_g[2][:, 0:1024].bitcast(I32)
        gws = gate_g[2][:, 1024:2048]
        mask = [gate_g[2][:, 2048 + 1024 * i:3072 + 1024 * i] for i in range(2)]
        tbuf = sb("tbuf", [P, H // 2 * L])
        toep = tbuf[:, :].rearrange("p (h l) -> p h l", l=L)
        hid = [tbuf[:, 512 * i:512 * i + 512] for i in range(FB)]
        turn = [tbuf[:, 2048 + 512 * i:2560 + 512 * i] for i in range(FB)]
        xs = sb("xs", [P, T])
        scr = sb("scr", [P, 7168])
        xrev = scr[:, 0:2048]
        gsum = scr[:, 2048:4096]
        y_gelu = scr[:, 4096:6144]
        w1_raw = scr[:, 6144:6656]
        w2_raw = scr[:, 6656:7168]
        gated = [scr[:, 512 * i:512 * i + 512] for i in range(RING)]
        whole = [scr[:, 2048 + 512 * i:2560 + 512 * i] for i in range(2)]
        xn2 = [scr[:, 3072 + 512 * i:3584 + 512 * i] for i in range(2)]
        o_sb = scr[:, 6144:6656]
        y_sb = scr[:, 6656:7168]
        fin = scr[:, 5120:5632]
        y_t = [scr[:, 4096 + 512 * i:4608 + 512 * i] for i in range(2)]
        xt_h, xt_l = sb("xt_h", [P, T], F32R), sb("xt_l", [P, T], F32R)
        win_h, win_l = sb("win_h", [P, NB * P], F32R), sb("win_l", [P, NB * P], F32R)
        wout_h, wout_l = sb("wout_h", [P, NB * P], F32R), sb("wout_l", [P, NB * P], F32R)
        w1_h, w1_l = sb("w1_h", [P, F], F32R), sb("w1_l", [P, F], F32R)
        w2_h, w2_l = sb("w2_h", [P, F], F32R), sb("w2_l", [P, F], F32R)
        hb_h, hb_l = sb("hb_h", [P, RING, GT], F32R), sb("hb_l", [P, RING, GT], F32R)
        x2_h, x2_l = sb("x2_h", [P, GT], F32R), sb("x2_l", [P, GT], F32R)
        AR = 3
        act_h, act_l = sb("act_h", [P, AR, GT], F32R), sb("act_l", [P, AR, GT], F32R)
        ones = sb("ones", [P, P])
        ident = sb("ident", [P, P])
        pairs = sb("pairs", [P, 32])
        nhalf = sb("nhalf", [P, TG])
        warm = sb("warm", [P, 1])
        kp = sb("kp", [P, 2 * L])
        fc = sb("fc", [P, 4 * FB + 1])
        s4 = sb("s4", [P, 4 * N + 2])
        ar, ai, cr, ci = (s4[:, N * i:N * i + N] for i in range(4))
        ldt, dsk = s4[:, 4 * N:4 * N + 1], s4[:, 4 * N + 1:4 * N + 2]
        NA = N + FB
        ang, kturn, rest, sn, sh, cs, tq = (sb(n, [P, NA]) for n in ("ang", "kturn", "rest", "sn", "sh", "cs", "tq"))
        dt_ = sb("dt_", [P, 1])
        ea, dre, mag, zm, are, den, inv, t0, t1, t2, t3, nr, ni = (
            sb(n, [P, N]) for n in ("ea", "dre", "mag", "zm", "are", "den", "inv", "t0", "t1", "t2", "t3", "nr", "ni"))
        qpow = sb("qpow", [P, 8 * 2 * N])
        ppow = sb("ppow", [P, 8 * 2 * N])
        zhi = sb("zhi", [P, 3 * 2 * N])
        td = sb("td", [P, 3 * 2 * N])
        te = sb("te", [P, 3 * 2 * N])
        tp = sb("tp", [P, 4 * 2 * N])
        tr = sb("tr", [P, 4 * 2 * N])
        cff, tbias = sb("cff", [P, FB]), sb("tbias", [P, FB])
        stat = [sb(f"stat{i}", [P, TG, 6]) for i in range(3)]
        mv = [sb(f"mv{i}", [P, TG, 2]) for i in range(3)]
        ve = [sb(f"ve{i}", [P, TG]) for i in range(3)]
        rs = [sb(f"rs{i}", [P, TG]) for i in range(3)]
        nmean, shift = sb("nmean", [P, TG]), sb("shift", [P, TG])

        bank = ctx.enter_context(nc.psum_tensor("bank", [P, 8, 512], F32))
        o_ps, y_ps = bank[:, 0, :], bank[:, 3, :]
        f_ps = [bank[:, 1, :], bank[:, 2, :]]
        h_ps = [bank[:, 4, :], bank[:, 5, :]]
        ta_ps, tb_ps = bank[:, 6, :], bank[:, 7, :]

        names = """par ids gws xrev x win wout w1 w2 ffn kpad ystore gstore store
            cst exp dre mag rest sin zm zhi inv den pp pq red kp qpow
            whi wlo mask gsum gev conv gelu yturn z1 var1 rstd1 xn1 xt xth xtl
            in gated hi lo out oev ot z2 var2 rstd2 xn2 x2t x2h x2l
            fin turn fev frac sine mix ah al fout yev yt z3 var3 rstd3 res dchain pchain"""
        S = {n: sem("s_" + n) for n in names.split()}
        s_toep = [sem(f"s_toep{c}") for c in range(4)]
        s_gate = [[sem(f"s_gate{g}_{i}") for i in range(2)] for g in range(G)]
        s_yload = [sem(f"s_yload{g}") for g in range(G)]
        s_var, s_rstd = [S["var1"], S["var2"], S["var3"]], [S["rstd1"], S["rstd2"], S["rstd3"]]

        def grp(t, g):
            return t[:, g * GT:(g + 1) * GT]

        def due(stage, t):
            if stage in PER_BLOCK:
                g, f = divmod(t - SLOTS[stage], NB)
                return FB * g + f if 0 <= g < G and f < FB else None
            g, rem = divmod(t - SLOTS[stage], NB)
            return g if rem == 0 and (1 if SLOTS[stage] < 0 else 0) <= g < G else None

        LAST_SLOT = NB * (G - 1) + SLOTS["norm3"]
        block = ctx.enter_context(nc.Block())

        @block.sync
        def _(sp):
            sp.dma_start(s4[:, :], s4d_par).then_inc(S["par"], 16)
            sp.dma_start(fc[:, :], ffn_par).then_inc(S["ffn"], 16)
            sp.dma_start(ids, gate_id).then_inc(S["ids"], 16)
            sp.dma_start(gws, gate_w).then_inc(S["gws"], 16)
            sp.dma_start(xrev, x_rev).then_inc(S["xrev"], 16)
            sp.dma_start(xs[:, :], x).then_inc(S["x"], 16)
            sp.wait_ge(S["kp"], 1)
            sp.dma_start(kpad, kp[:, :]).then_inc(S["kpad"], 16)
            sp.wait_ge(S["kpad"], 16)
            for c in range(2):
                for r in range(2):
                    q = 2 * r + c
                    sp.dma_start(toep[L * r:L * r + L, HQ * c:HQ * c + HQ, :],
                                 bass.AP(kpad.tensor, 1 + q * HQ * 2 * L, [[1, L], [2 * L, HQ], [1, L]])) \
                        .then_inc(s_toep[2 * c + r], 16)
            sp.wait_ge(S["gev"], 2)
            for j in range(4):
                sp.dma_start(bass.AP(gates.tensor, j * T, [[T // 2, 2], [4 * T, 2], [1, T // 2]]),
                             gsum[32 * j:32 * j + 2, :].rearrange("q (a t) -> q a t", a=2)).then_inc(S["gstore"], 16)
            sp.wait_ge(S["gelu"], 2)
            for j in range(JC):
                sp.dma_start(bass.AP(y_dram.tensor, j * 2 * HH * L, [[H * L, B], [1, 2 * HH * L]]),
                             y_gelu[32 * j:32 * j + 32, :]).then_inc(S["ystore"], 16)
            sp.wait_ge(S["gstore"], 64)

            def load_gates(g, i):
                if g >= NGB:
                    sp.wait_ge(S["gated"], NB * (g - NGB + 1))
                half = E // 2
                sp.dma_start(gate_g[g % NGB][:, i * half * GT:(i + 1) * half * GT]
                             .rearrange("p (e t) -> p e t", e=half),
                             bass.AP(gates.tensor, i * half * T + g * GT, [[0, P], [T, half], [1, GT]])) \
                    .then_inc(s_gate[g][i], 16)

            def load_y(g):
                if g >= 2:
                    sp.wait_ge(S["yturn"], g - 1)
                sp.dma_start(y_t[g % 2].rearrange("h (b l) -> h b l", l=L),
                             bass.AP(y_dram.tensor, g * BG * H * L, [[L, H], [H * L, BG], [1, L]])) \
                    .then_inc(s_yload[g], 16)

            sp.wait_ge(S["red"], 1)
            load_gates(0, 0)
            sp.wait_ge(S["ystore"], 64)
            load_y(0)
            load_gates(0, 1)
            load_y(1)
            sp.wait_ge(S["wlo"], 10)
            load_gates(1, 0)
            load_gates(1, 1)
            load_y(2)
            sp.wait_ge(S["gsum"], 16)
            load_gates(2, 0)
            load_gates(2, 1)
            load_y(3)
            load_gates(3, 0)
            load_gates(3, 1)
            for g in range(G):
                sp.wait_ge(S["res"], g + 1)
                sp.dma_start(grp(out, g), fin).then_inc(S["store"], 16)
            sp.wait_ge(S["store"], 16 * G)

        @block.gpsimd
        def _(pool):
            chain = [0]

            def link(ins):
                chain[0] += 1
                ins.then_inc(S["pchain"], 1)
                pool.wait_ge(S["pchain"], chain[0])

            tt = nc.gpsimd.tensor_tensor
            nc.gpsimd.memset(pairs[:, :], 0.0).then_inc(S["cst"], 1)
            nc.gpsimd.memset(nhalf[:, :], -0.5).then_inc(S["cst"], 1)
            link(nc.gpsimd.memset(ones[:, :], 1.0))
            pool.wait_ge(S["cst"], 2)
            nc.gpsimd.affine_select(out=ident[:, :], in_=ones[:, :], compare_op=ALU.is_equal, fill=0.0,
                                    base=0, pattern=[[-1, P]], channel_multiplier=1).then_inc(S["cst"], 1)
            pool.wait_ge(S["cst"], 3)
            for q in range(2):
                nc.gpsimd.memset(pairs[L * q:L * q + L, q:q + 1], 1.0).then_inc(S["cst"], 1)
                pool.wait_ge(S["cst"], 4 + q)

            pool.wait_ge(S["par"], 16)
            pool.wait_ge(S["exp"], 1)
            nc.gpsimd.tensor_scalar(are[:, :], ea[:, :], -1.0, None, ALU.mult)
            tt(t0[:, :], ea[:, :], ea[:, :], ALU.mult)
            link(tt(t1[:, :], ai, ai, ALU.mult))
            link(tt(den[:, :], t0[:, :], t1[:, :], ALU.add))
            nc.gpsimd.tensor_scalar(den[:, :], den[:, :], 0.5, None, ALU.mult).then_inc(S["den"], 1)
            pool.wait_ge(S["zm"], 1)
            zc = qpow[:, 3 * N:4 * N]
            tt(t0[:, :], cr, zm[:, :], ALU.mult)
            tt(t1[:, :], ci, zc, ALU.mult)
            tt(t2[:, :], ci, zm[:, :], ALU.mult)
            link(tt(t3[:, :], cr, zc, ALU.mult))
            tt(nr[:, :], t0[:, :], t1[:, :], ALU.add)
            link(tt(ni[:, :], t2[:, :], t3[:, :], ALU.subtract))
            tt(t0[:, :], nr[:, :], are[:, :], ALU.mult)
            tt(t1[:, :], ni[:, :], ai, ALU.mult)
            tt(t2[:, :], ni[:, :], are[:, :], ALU.mult)
            link(tt(t3[:, :], nr[:, :], ai, ALU.mult))
            tt(nr[:, :], t0[:, :], t1[:, :], ALU.add)
            link(tt(ni[:, :], t2[:, :], t3[:, :], ALU.subtract))
            pool.wait_ge(S["inv"], 1)
            tt(ppow[:, 0:N], nr[:, :], inv[:, :], ALU.mult)
            link(tt(ppow[:, N:2 * N], ni[:, :], inv[:, :], ALU.mult))
            for i, m in enumerate((1, 2, 4)):
                pool.wait_ge(S["zhi"], i + 1)
                src = ppow[:, 0:2 * N * m]
                yr = zhi[:, 2 * N * i:2 * N * i + N]
                yc = zhi[:, 2 * N * i + N:2 * N * i + 2 * N]
                s3 = [[2 * N, m], [N, 2], [1, N]]
                tt(view(tp[:, :], s3), view(src, s3), view(yr, [[0, m], [0, 2], [1, N]]), ALU.mult)
                link(tt(view(tr[:, :], s3), view(src, s3), view(yc, [[0, m], [0, 2], [1, N]]), ALU.mult))
                dst = ppow[:, 2 * N * m:4 * N * m]
                s2 = [[2 * N, m], [1, N]]
                tt(view(dst, s2), view(tp[:, :], s2), view(tr[:, :], s2, N), ALU.add)
                tt(view(dst, s2, N), view(tp[:, :], s2, N), view(tr[:, :], s2), ALU.subtract).then_inc(S["pp"], 1)
                pool.wait_ge(S["pp"], i + 1)
            pool.wait_ge(S["qpow"], 1)
            share = prod[:, 6 * 16 * N:8 * 16 * N]
            link(tt(view(share, [[16 * N, 2], [2 * N, 8], [1, 2 * N]]),
                    view(ppow[:, :], [[2 * N, 2], [0, 8], [1, 2 * N]], 12 * N),
                    view(qpow[:, :], [[0, 2], [2 * N, 8], [1, 2 * N]]), ALU.mult))
            tt(view(share, [[2 * N, 16], [1, N]]), view(share, [[2 * N, 16], [1, N]]),
               view(share, [[2 * N, 16], [1, N]], N), ALU.add).then_inc(S["pq"], 1)

            def weight_low(dst, raw, high, w, i):
                tt(dst[:, w], raw[:, w], high[:, w].bitcast(F32), ALU.subtract).then_inc(S["wlo"], 1)

            i = 0
            for dst, raw, high, count in ((win_l, win_raw, win_h, 4), (wout_l, wout_raw, wout_h, 4),
                                          (w1_l, w1_raw, w1_h, 1), (w2_l, w2_raw, w2_h, 1)):
                pool.wait_ge(S["whi"], {4: 1 + (dst is wout_l), 1: 3 + (dst is w2_l)}[count])
                for c in range(count):
                    weight_low(dst, raw, high, slice(512 * c, 512 * c + 512), i)
                    i += 1

            def inv_std(k, g):
                pool.wait_ge(s_var[k], g + 1)
                if k == 0:
                    link(tt(rs[0][:, :], ve[0][:, :], nhalf[:, :], ALU.pow))
                    tt(shift[:, :], nmean[:, :], rs[0][:, :], ALU.mult).then_inc(s_rstd[0], 1)
                else:
                    tt(rs[k][:, :], ve[k][:, :], nhalf[:, :], ALU.pow).then_inc(s_rstd[k], 1)

            def low(n):
                pool.wait_ge(S["hi"], n + 1)
                if n >= RING:
                    pool.wait_ge(S["out"], n - RING + 1)
                tt(hb_l[:, n % RING, :], gated[n % RING], hb_h[:, n % RING, :].bitcast(F32), ALU.subtract) \
                    .then_inc(S["lo"], 1)

            inv_std(0, 0)
            for t in range(LAST_SLOT + 1):
                for k in range(3):
                    g = due(f"rstd{k + 1}", t)
                    if g is not None:
                        inv_std(k, g)
                if t < NB * G:
                    low(t)

        @block.scalar
        def _(act):
            av = nc.scalar.activation
            act.dma_start(win_raw, w_in).then_inc(S["win"], 16)
            act.dma_start(wout_raw, w_out).then_inc(S["wout"], 16)
            act.dma_start(w1_raw, w1).then_inc(S["w1"], 16)
            act.dma_start(w2_raw, w2).then_inc(S["w2"], 16)
            act.wait_ge(S["cst"], 5)
            av(warm[:, :], nhalf[:, 0:1], ACT.Exp)
            act.wait_ge(S["par"], 16)
            av(dt_[:, :], ldt, ACT.Exp)
            av(ea[:, :], ar, ACT.Exp).then_inc(S["exp"], 1)
            act.wait_ge(S["dre"], 1)
            av(mag[:, :], dre[:, :], ACT.Exp).then_inc(S["mag"], 1)
            act.wait_ge(S["rest"], 1)
            av(sn[:, :], rest[:, :], ACT.Sin)
            av(sh[:, :], rest[:, :], ACT.Sin, scale=0.5).then_inc(S["sin"], 1)
            for arrived, dst, raw in (("win", win_h, win_raw), ("wout", wout_h, wout_raw), ("w1", w1_h, w1_raw),
                                      ("w2", w2_h, w2_raw)):
                act.wait_ge(S[arrived], 16)
                av(dst[:, :], raw, ACT.Copy).then_inc(S["whi"], 1)
            for a in range(2):
                act.wait_ge(S["gsum"], 8 * (a + 1))
                av(gsum[:, 1024 * a:1024 * a + 1024], bank[:, 4 + 2 * a:6 + 2 * a, :].rearrange("p a b -> p (a b)"),
                   ACT.Copy).then_inc(S["gev"], 1)
            for c in range(2):
                act.wait_ge(S["conv"], c + 1)
                av(view(y_gelu, [[2 * GT, 2], [1, GT]], c * GT), bank[:, 2 * c:2 * c + 2, :], ACT.Gelu) \
                    .then_inc(S["gelu"], 1)

            def norm1(g):
                act.wait_ge(s_rstd[0], g + 1)
                for c in range(TG):
                    o = g * GT + c * P
                    last = av(xs[:, o:o + P], xs[:, o:o + P], ACT.Identity, bias=shift[:, c:c + 1],
                              scale=rs[0][:, c:c + 1])
                last.then_inc(S["xn1"], 1)

            def xt_high(g):
                act.wait_ge(S["xt"], g + 1)
                av(grp(xt_h, g), ta_ps, ACT.Copy).then_inc(S["xth"], 1)

            norm1(0)
            xt_high(0)

            def high(n):
                act.wait_ge(S["gated"], n + 1)
                if n >= RING:
                    act.wait_ge(S["out"], n - RING + 1)
                av(hb_h[:, n % RING, :], gated[n % RING], ACT.Copy).then_inc(S["hi"], 1)

            def f_parts(m):
                f = m % FB
                act.wait_ge(S["fin"], m + 1)
                if m >= FB:
                    act.wait_ge(S["al"], m - FB + 1)
                av(turn[f], f_ps[m % 2], ACT.Identity, bias=tbias[:, f:f + 1], scale=0.1 * INV_TWO_PI) \
                    .then_inc(S["turn"], 1)
                av(hid[f], f_ps[m % 2], ACT.Identity, bias=fc[:, 3 * FB + f:3 * FB + f + 1])
                act.wait_ge(S["turn"], m + 1)
                if m >= 2:
                    act.wait_ge(S["frac"], m - 1)
                av(whole[m % 2], turn[f], ACT.Copy, bias=ROUND).then_inc(S["fev"], 1)

            def f_sine(m):
                act.wait_ge(S["frac"], m + 1)
                av(turn[m % FB], turn[m % FB], ACT.Sin, scale=-TWO_PI_BELOW).then_inc(S["sine"], 1)

            def f_high(m):
                act.wait_ge(S["mix"], m + 1)
                if m >= AR:
                    act.wait_ge(S["fout"], m - AR + 1)
                av(act_h[:, m % AR, :], hid[m % FB], ACT.Relu).then_inc(S["ah"], 1)

            for t in range(LAST_SLOT + 1):
                if t < NB * G:
                    high(t)
                if (g := due("o_evac", t)) is not None:
                    act.wait_ge(S["out"], NB * (g + 1))
                    if g >= 1:
                        act.wait_ge(S["ot"], g)
                    av(o_sb, o_ps, ACT.Copy).then_inc(S["oev"], 1)
                if (g := due("norm1", t)) is not None:
                    norm1(g)
                if (g := due("xt_high", t)) is not None:
                    xt_high(g)
                if (g := due("x2_high", t)) is not None:
                    act.wait_ge(S["x2t"], g + 1)
                    if g >= 1:
                        act.wait_ge(S["fin"], FB * g)
                    av(x2_h[:, :], tb_ps, ACT.Copy).then_inc(S["x2h"], 1)
                if (m := due("f_high", t)) is not None:
                    f_high(m)
                if (m := due("f_sine", t)) is not None:
                    f_sine(m)
                if (m := due("f_parts", t)) is not None:
                    f_parts(m)
                if (g := due("y_evac", t)) is not None:
                    act.wait_ge(S["fout"], FB * (g + 1))
                    if g >= 1:
                        act.wait_ge(S["yt"], g)
                    av(y_sb, y_ps, ACT.Identity, bias=fc[:, 4 * FB:4 * FB + 1]).then_inc(S["yev"], 1)

        @block.vector
        def _(dve):
            chain = [0]

            def link(ins):
                chain[0] += 1
                ins.then_inc(S["dchain"], 1)
                dve.wait_ge(S["dchain"], chain[0])

            tt, ts, stt = nc.vector.tensor_tensor, nc.vector.tensor_scalar, nc.vector.scalar_tensor_tensor
            nc.vector.memset(kp[:, 0:L], 0.0)
            nc.vector.memset(qpow[:, 0:N], 1.0)
            link(nc.vector.memset(qpow[:, N:2 * N], 0.0))
            dve.wait_ge(S["par"], 16)
            dve.wait_ge(S["ffn"], 16)
            nc.vector.tensor_copy(ang[:, N:NA], fc[:, 0:FB])
            dve.wait_ge(S["exp"], 1)
            ts(dre[:, :], ea[:, :], dt_[:, 0:1], -1.0, ALU.mult, ALU.mult).then_inc(S["dre"], 1)
            link(ts(ang[:, 0:N], ai, dt_[:, 0:1], None, ALU.mult))
            link(ts(kturn[:, :], ang[:, :], INV_TWO_PI, ROUND, ALU.mult, ALU.add))
            link(ts(kturn[:, :], kturn[:, :], ROUND, None, ALU.subtract))
            link(stt(rest[:, :], kturn[:, :], -TWO_PI_HI, ang[:, :], ALU.mult, ALU.add))
            link(stt(rest[:, :], kturn[:, :], -TWO_PI_LO, rest[:, :], ALU.mult, ALU.add))
            ts(rest[:, :], rest[:, :], PI_BELOW, -PI_BELOW, ALU.min, ALU.max).then_inc(S["rest"], 1)
            dve.wait_ge(S["den"], 1)
            nc.vector.reciprocal(inv[:, :], den[:, :]).then_inc(S["inv"], 1)
            dve.wait_ge(S["sin"], 1)
            link(tt(cs[:, :], sh[:, :], sh[:, :], ALU.mult))
            link(ts(cs[:, :], cs[:, :], -2.0, 1.0, ALU.mult, ALU.add))
            dve.wait_ge(S["mag"], 1)
            z1 = qpow[:, 2 * N:4 * N]
            tt(z1[:, 0:N], mag[:, :], cs[:, 0:N], ALU.mult)
            link(stt(z1[:, N:2 * N], mag[:, :], -1.0, sn[:, 0:N], ALU.mult, ALU.mult))
            ts(zm[:, :], z1[:, 0:N], -1.0, None, ALU.add).then_inc(S["zm"], 1)

            def square(dst, src):
                tt(td[:, 0:2 * N], src, src, ALU.mult)
                link(stt(dst[:, N:2 * N], src[:, 0:N], 2.0, src[:, N:2 * N], ALU.mult, ALU.mult))
                return tt(dst[:, 0:N], td[:, 0:N], td[:, N:2 * N], ALU.subtract)

            def times(dst, src, by, m):
                s3 = [[2 * N, m], [N, 2], [1, N]]
                tt(view(td[:, :], s3), view(src, s3), view(by[:, 0:N], [[0, m], [0, 2], [1, N]]), ALU.mult)
                link(tt(view(te[:, :], s3), view(src, s3), view(by[:, N:2 * N], [[0, m], [0, 2], [1, N]]), ALU.mult))
                s2 = [[2 * N, m], [1, N]]
                tt(view(dst, s2), view(td[:, :], s2), view(te[:, :], s2, N), ALU.subtract)
                return tt(view(dst, s2, N), view(td[:, :], s2, N), view(te[:, :], s2), ALU.add)

            def q_(c, m=1):
                return qpow[:, 2 * N * c:2 * N * (c + m)]

            link(square(q_(2), q_(1)))
            link(square(q_(4), q_(2)))
            for i in range(3):
                square(zhi[:, 2 * N * i:2 * N * (i + 1)], q_(4) if i == 0 else zhi[:, 2 * N * (i - 1):2 * N * i]) \
                    .then_inc(S["zhi"], 1)
                dve.wait_ge(S["zhi"], i + 1)
            link(times(q_(3), q_(2), q_(1), 1))
            times(q_(5, 3), q_(1, 3), q_(4), 3).then_inc(S["qpow"], 1)
            dve.wait_ge(S["qpow"], 1)
            tt(tq[:, 0:FB], cs[:, N:NA], fc[:, FB:2 * FB], ALU.mult)
            link(tt(kturn[:, 0:FB], sn[:, N:NA], fc[:, 2 * FB:3 * FB], ALU.mult))
            link(tt(tq[:, 0:FB], tq[:, 0:FB], kturn[:, 0:FB], ALU.add))
            stt(cff[:, :], tq[:, 0:FB], 0.1, fc[:, 2 * FB:3 * FB], ALU.mult, ALU.mult)
            link(ts(tbias[:, :], rest[:, N:NA], INV_TWO_PI, None, ALU.mult))
            link(stt(tbias[:, :], fc[:, 3 * FB:4 * FB], 0.1 * INV_TWO_PI, tbias[:, :], ALU.mult, ALU.add))
            for a, m, need in ((0, 4, 2), (4, 2, 3)):
                dve.wait_ge(S["pp"], need)
                part = prod[:, 16 * N * a:16 * N * (a + m)]
                link(tt(view(part, [[16 * N, m], [2 * N, 8], [1, 2 * N]]),
                        view(ppow[:, :], [[2 * N, m], [0, 8], [1, 2 * N]], 2 * N * a),
                        view(qpow[:, :], [[0, m], [2 * N, 8], [1, 2 * N]]), ALU.mult))
                nc.vector.tensor_reduce(kp[:, L + 8 * a:L + 8 * (a + m)], part.rearrange("p (l n) -> p l n", n=2 * N),
                                        AX_X, ALU.add)
            dve.wait_ge(S["pq"], 1)
            nc.vector.tensor_reduce(kp[:, L + 48:L + 64], view(prod[:, 6 * 16 * N:8 * 16 * N], [[2 * N, 16], [1, N]]),
                                    AX_X, ALU.add).then_inc(S["red"], 1)
            dve.wait_ge(S["red"], 1)
            ts(kp[:, L:L + 1], kp[:, L:L + 1], dsk, None, ALU.add).then_inc(S["kp"], 1)

            dve.wait_ge(S["ids"], 16)
            dve.wait_ge(S["gws"], 16)
            for e in range(E):
                if e >= 2:
                    dve.wait_ge(S["gsum"], 2 * (e - 1))
                stt(mask[e % 2], ids, float(e), gws, ALU.is_equal, ALU.mult).then_inc(S["mask"], 1)

            def spread(src, k):
                for c in range(TG):
                    last = nc.vector.bn_stats(stat[k][:, c, :], src[:, c * P:(c + 1) * P])
                link(last)
                for c in range(TG):
                    last = nc.vector.bn_aggr(mv[k][:, c, :], stat[k][:, c, :])
                link(last)
                if k == 0:
                    ts(nmean[:, :], view(mv[k][:, 0, :], [[2, TG]]), -1.0, None, ALU.mult)
                ts(ve[k][:, :], view(mv[k][:, 0, :], [[2, TG]], 1), EPS, None, ALU.add).then_inc(s_var[k], 1)

            def normalise(dst, src, k, g, done):
                dve.wait_ge(s_rstd[k], g + 1)
                for c in range(TG):
                    last = ts(dst[:, c * P:(c + 1) * P], src[:, c * P:(c + 1) * P], mv[k][:, c, 0:1],
                              rs[k][:, c:c + 1], ALU.subtract, ALU.mult)
                last.then_inc(done, 1)

            def add_gelu(g):
                dve.wait_ge(S["yturn"], g + 1)
                if g == 0:
                    dve.wait_ge(S["x"], 16)
                tt(grp(xs, g), ta_ps, grp(xs, g), ALU.add).then_inc(S["z1"], 1)
                dve.wait_ge(S["z1"], g + 1)
                spread(grp(xs, g), 0)

            def xt_low(g):
                dve.wait_ge(S["xth"], g + 1)
                tt(grp(xt_l, g), ta_ps, grp(xt_h, g).bitcast(F32), ALU.subtract).then_inc(S["xtl"], 1)

            add_gelu(0)
            xt_low(0)

            def gate_block(n):
                g, j = divmod(n, NB)
                if j % (NB // 2) == 0:
                    dve.wait_ge(s_gate[g][j // (NB // 2)], 16)
                dve.wait_ge(S["in"], n + 1)
                if n >= RING:
                    dve.wait_ge(S["hi"], n - RING + 1)
                    dve.wait_ge(S["lo"], n - RING + 1)
                e = j // DH
                stt(gated[n % RING], h_ps[n % 2], 0.0, gate_g[g % NGB][:, e * GT:(e + 1) * GT],
                    ALU.max, ALU.mult).then_inc(S["gated"], 1)

            def f_frac(m):
                dve.wait_ge(S["fev"], m + 1)
                stt(turn[m % FB], whole[m % 2], ROUND, turn[m % FB], ALU.subtract, ALU.subtract) \
                    .then_inc(S["frac"], 1)

            def f_mix(m):
                f = m % FB
                dve.wait_ge(S["sine"], m + 1)
                stt(hid[f], turn[f], cff[:, f:f + 1], hid[f], ALU.mult, ALU.add).then_inc(S["mix"], 1)

            def f_low(m):
                dve.wait_ge(S["ah"], m + 1)
                if m >= AR:
                    dve.wait_ge(S["fout"], m - AR + 1)
                stt(act_l[:, m % AR, :], hid[m % FB], 0.0, act_h[:, m % AR, :].bitcast(F32),
                    ALU.max, ALU.subtract).then_inc(S["al"], 1)

            for t in range(LAST_SLOT + 1):
                if t < NB * G:
                    gate_block(t)
                if (g := due("z1", t)) is not None:
                    add_gelu(g)
                if (g := due("xt_low", t)) is not None:
                    xt_low(g)
                if (g := due("z2", t)) is not None:
                    dve.wait_ge(S["ot"], g + 1)
                    tt(xn2[g % 2], tb_ps, grp(xs, g), ALU.add).then_inc(S["z2"], 1)
                    dve.wait_ge(S["z2"], g + 1)
                    spread(xn2[g % 2], 1)
                if (g := due("norm2", t)) is not None:
                    normalise(xn2[g % 2], xn2[g % 2], 1, g, S["xn2"])
                if (g := due("x2_low", t)) is not None:
                    dve.wait_ge(S["x2h"], g + 1)
                    if g >= 1:
                        dve.wait_ge(S["fin"], FB * g)
                    tt(x2_l[:, :], tb_ps, x2_h[:, :].bitcast(F32), ALU.subtract).then_inc(S["x2l"], 1)
                if (m := due("f_low", t)) is not None:
                    f_low(m)
                if (m := due("f_mix", t)) is not None:
                    f_mix(m)
                if (m := due("f_frac", t)) is not None:
                    f_frac(m)
                if (g := due("z3", t)) is not None:
                    dve.wait_ge(S["yt"], g + 1)
                    if g >= 1:
                        dve.wait_ge(S["store"], 16 * g)
                    tt(fin, ta_ps, xn2[g % 2], ALU.add).then_inc(S["z3"], 1)
                    dve.wait_ge(S["z3"], g + 1)
                    spread(fin, 2)
                if (g := due("norm3", t)) is not None:
                    normalise(fin, fin, 2, g, S["res"])

        @block.tensor
        def _(pe):
            mm = nc.tensor.matmul
            pe.wait_ge(S["cst"], 5)
            for e in range(E):
                pe.wait_ge(S["mask"], e + 1)
                for i in range(2):
                    mm(bank[32 * (e % 4):32 * (e % 4) + 32, 4 + 2 * (e // 4) + i, :], pairs[:, :],
                       mask[e % 2][:, i * 512:(i + 1) * 512], start=True, stop=True).then_inc(S["gsum"], 1)
            pe.wait_ge(S["xrev"], 16)
            xr = xrev.rearrange("p (b h) -> p h b", b=B)
            for c in range(2):
                pe.wait_ge(s_toep[2 * c], 16)
                pe.wait_ge(s_toep[2 * c + 1], 16)
                for i in range(HH // 2):
                    for r in range(2):
                        for j in range(JC):
                            last = mm(bank[32 * j:32 * j + 32, 2 * c + r, i * L:(i + 1) * L],
                                      xr[L * r:L * r + L, HH * j + HH // 2 * c + i, :],
                                      toep[L * r:L * r + L, HQ * c + HH // 2 * j + i, :], start=True, stop=True)
                last.then_inc(S["conv"], 1)

            def three(dst, wh, wl, vh, vl, first, last):
                mm(dst, wh, vh, start=first, stop=False)
                mm(dst, wl, vh, start=False, stop=False)
                return mm(dst, wh, vl, start=False, stop=last)

            def turn4(dst, src, done):
                for c in range(TG):
                    last = nc.tensor.transpose(dst[:, c * P:(c + 1) * P], src[:, c * P:(c + 1) * P], ident[:, :])
                last.then_inc(S[done], 1)

            def y_turn(g):
                pe.wait_ge(s_yload[g], 16)
                turn4(ta_ps, y_t[g % 2], "yturn")

            def xt_turn(g):
                pe.wait_ge(S["xn1"], g + 1)
                turn4(ta_ps, grp(xs, g), "xt")

            pe.wait_ge(S["gev"], 2)
            y_turn(0)
            xt_turn(0)
            pe.wait_ge(S["wlo"], 10)

            def first_product(n):
                g, j = divmod(n, NB)
                if j == 0:
                    pe.wait_ge(S["xtl"], g + 1)
                if n >= 2:
                    pe.wait_ge(S["gated"], n - 1)
                w = slice(j * P, (j + 1) * P)
                three(h_ps[n % 2], win_h[:, w], win_l[:, w], grp(xt_h, g), grp(xt_l, g), True, True) \
                    .then_inc(S["in"], 1)

            def second_product(n):
                g, j = divmod(n, NB)
                if n == 0:
                    pe.wait_ge(S["gelu"], 2)
                if j == 0 and g >= 1:
                    pe.wait_ge(S["oev"], g)
                pe.wait_ge(S["lo"], n + 1)
                w = slice(j * P, (j + 1) * P)
                r = n % RING
                three(o_ps, wout_h[:, w], wout_l[:, w], hb_h[:, r, :], hb_l[:, r, :], j == 0, j == NB - 1) \
                    .then_inc(S["out"], 1)

            def f_first(m):
                f = m % FB
                if f == 0:
                    pe.wait_ge(S["x2l"], m // FB + 1)
                if m >= 2:
                    pe.wait_ge(S["fev"], m - 1)
                w = slice(f * P, (f + 1) * P)
                three(f_ps[m % 2], w1_h[:, w], w1_l[:, w], x2_h[:, :], x2_l[:, :], True, True) \
                    .then_inc(S["fin"], 1)

            def f_second(m):
                f = m % FB
                if f == 0 and m >= FB:
                    pe.wait_ge(S["yev"], m // FB)
                pe.wait_ge(S["al"], m + 1)
                w = slice(f * P, (f + 1) * P)
                r = m % AR
                three(y_ps, w2_h[:, w], w2_l[:, w], act_h[:, r, :], act_l[:, r, :], f == 0, f == FB - 1) \
                    .then_inc(S["fout"], 1)

            for t in range(LAST_SLOT + 1):
                if t < NB * G:
                    first_product(t)
                if LAG <= t < NB * G + LAG:
                    second_product(t - LAG)
                if (g := due("y_turn", t)) is not None:
                    pe.wait_ge(S["xtl"], g)
                    y_turn(g)
                if (g := due("out_turn", t)) is not None:
                    if g + 2 < G:
                        pe.wait_ge(S["z1"], g + 3)
                    pe.wait_ge(S["yev"], g + 1)
                    turn4(ta_ps, y_sb, "yt")
                if (g := due("xt_turn", t)) is not None:
                    if g >= 3:
                        pe.wait_ge(S["z3"], g - 2)
                    xt_turn(g)
                if (g := due("o_turn", t)) is not None:
                    pe.wait_ge(S["oev"], g + 1)
                    if g >= 1:
                        pe.wait_ge(S["x2l"], g)
                    turn4(tb_ps, o_sb, "ot")
                if (g := due("x2_turn", t)) is not None:
                    pe.wait_ge(S["xn2"], g + 1)
                    turn4(tb_ps, xn2[g % 2], "x2t")
                if (m := due("f_first", t)) is not None:
                    f_first(m)
                if (m := due("f_second", t)) is not None:
                    f_second(m)


def kernel(**inputs):
    import numpy as _np
    import concourse.bacc as _bacc
    from concourse import mybir as _mybir
    from concourse.bass_utils import run_bass_kernel_spmd as _run

    a = {k: _np.asarray(v) for k, v in inputs.items()}
    x = a['x']
    b, l, h = x.shape
    t = b * l
    experts, d, _ = a['L0_xattn_proj_in'].shape
    f = a['L0_ffn_W1'].shape[1]

    def halves(v):
        return v.reshape(2, b // 2, l, l).transpose(0, 2, 1, 3).reshape(2 * l, t // 2)

    def blocks(v):
        return v.reshape(-1, 128).T

    laid = {
        "x": x.reshape(t // 128, 128, h).transpose(1, 0, 2).reshape(128, t),
        "x_rev": x[:, ::-1, :].reshape(b, l, 4, 2, 16).transpose(3, 1, 0, 2, 4).reshape(128, t),
        "gate_w": halves(a['ctx_512']),
        "gate_id": halves(a['itok_BxS2xS_0_7']),
        "s4d_par": _np.concatenate(
            [a['L0_attn_A_real'], a['L0_attn_A_imag'], a['L0_attn_C_real'], a['L0_attn_C_imag'],
             a['L0_attn_log_dt'].reshape(h, 1), _np.broadcast_to(a['L0_attn_D'].reshape(1, 1), (h, 1))], axis=1)
        .reshape(4, 2, 2, 8, -1).transpose(1, 2, 0, 3, 4).reshape(h, -1),
        "w_in": a['L0_xattn_proj_in'].transpose(2, 0, 1).reshape(h, experts * d),
        "w_out": a['L0_xattn_proj_out'].reshape(experts, h, d // 128, 128).transpose(3, 0, 2, 1)
        .reshape(128, experts * d),
        "w1": a['L0_ffn_W1'],
        "w2": a['L0_ffn_W2'].reshape(f // 128, 128, h).transpose(1, 0, 2).reshape(128, f),
        "ffn_par": _np.concatenate(
            [blocks(a['L0_ffn_quantum_phases']), blocks(a['L0_ffn_quantum_weights_real']),
             blocks(a['L0_ffn_quantum_weights_imag']), blocks(a['L0_ffn_b1']), blocks(a['L0_ffn_b2'])], axis=1),
    }
    nc = _bacc.Bacc("TRN2", target_bir_lowering=False, num_devices=1)
    arrays, args = {}, []
    for name, v in laid.items():
        v = _np.ascontiguousarray(v)
        arrays[f"in_{name}_dram"] = v
        args.append(nc.dram_tensor(f"in_{name}_dram", v.shape, _mybir.dt.from_np(v.dtype), kind="ExternalInput").ap())
    fp32 = _mybir.dt.float32
    args.append(nc.dram_tensor("kpad", (h, 2 * l), fp32, kind="Internal").ap())
    args.append(nc.dram_tensor("gates", (experts, t), fp32, kind="Internal").ap())
    args.append(nc.dram_tensor("y_dram", (b, h, l), fp32, kind="Internal").ap())
    args.append(nc.dram_tensor("out_0_dram", (128, t), fp32, kind="ExternalOutput").ap())
    s4d_moe_ffn_decoder(nc, *args)
    r = _run(nc, [arrays], core_ids=[0])
    got = r.results[0]["out_0_dram"]
    return got.reshape(128, t // 128, h).transpose(1, 0, 2).reshape(b, l, h)
```

```python
from contextlib import ExitStack

import concourse.bass as bass
from concourse import mybir

F32 = mybir.dt.float32
F32R = mybir.dt.float32r
I32 = mybir.dt.int32
ALU = mybir.AluOpType
ACT = mybir.ActivationFunctionType
AX_X = mybir.AxisListType.X

P = 128
TWO_PI_HI = 6.28125
TWO_PI_LO = 0.0019353071795864769
INV_TWO_PI = 0.15915494309189535
ROUND = 12582912.0
PI_BELOW = 3.1415925
TWO_PI_BELOW = 6.283185
EPS = 1e-5


def view(ap, dims, shift=0):
    return bass.AP(ap.tensor, ap.offset + shift, [list(ap.ap[0])] + [list(d) for d in dims])


SLOTS = {
    "y_turn": -14, "z1": -14, "stats1": -13, "var1": -12, "rstd1": -11, "norm1a": -8, "norm1b": -10,
    "xt_turn": -5, "xt_high": -5, "xt_low": -3,
    "o_evac": 19, "o_turn": 20, "z2": 21, "stats2": 21, "var2": 21, "rstd2": 21, "norm2": 23, "x2_turn": 25,
    "x2_high": 23, "x2_low": 26,
    "f_first": 27, "f_turn": 29, "f_hid": 30, "f_frac": 30, "f_sine": 31, "f_mix": 33, "f_high": 34,
    "f_low": 35, "f_second": 37,
    "y_evac": 51, "out_turn": 54, "z3": 53, "stats3": 56, "var3": 57, "rstd3": 59, "norm3": 60,
}
PER_BLOCK = {"f_first", "f_turn", "f_hid", "f_frac", "f_sine", "f_mix", "f_high", "f_low", "f_second"}
F_STEP = (4, 4, 2, 1)
LATE = {
    1: {"y_evac": 65, "out_turn": 67, "z3": 66, "stats3": 67, "var3": 71, "rstd3": 70, "norm3": 71},
    2: {"y_evac": 79, "out_turn": 82, "z3": 85, "stats3": 89, "var3": 90, "rstd3": 92, "norm3": 91},
    3: {"o_turn": 68, "z2": 68, "stats2": 68, "var2": 69, "rstd2": 69, "norm2": 70, "x2_turn": 73,
        "x2_high": 71, "x2_low": 72, "f_first": 74, "f_turn": 76, "f_hid": 77, "f_frac": 77, "f_sine": 78,
        "f_mix": 79, "f_high": 83, "f_low": 81, "f_second": 83, "y_evac": 91, "out_turn": 88, "z3": 91,
        "stats3": 93, "var3": 94, "rstd3": 95, "norm3": 96},
}


def s4d_moe_ffn_decoder(nc, x, x_rev, gate_w, gate_id, s4d_par, w_in, w_out, w1, w2, ffn_par,
                        kpad, gates, y_dram, out):
    T = x.shape[1]
    L = gate_w.shape[0] // 2
    H = x.shape[0]
    N = (s4d_par.shape[1] - 2) // 4
    B = T // L
    E, F = gates.shape[0], w1.shape[1]
    NB = w_in.shape[1] // P
    DH = NB // E
    GT = 512
    G = T // GT
    TG = GT // P
    TH = TG // 2
    BG = GT // L
    FB = F // P
    LAG = 4
    RING = 5
    JC = 4
    HH = H // 2 // JC
    PC = 4
    HI = HH // PC
    HQ = JC * HI
    assert H == P and L == 64 and B == 32 and FB == 4 and NB == 16 and G == 4 and N == 32 and E == 8

    with ExitStack() as ctx:
        def sb(name, shape, dt=F32):
            return ctx.enter_context(nc.sbuf_tensor(name, shape, dt))

        def sem(name):
            return ctx.enter_context(nc.semaphore(name))

        GS = E * GT
        NGB = 3
        gbuf = sb("gbuf", [P, NGB * GS])
        gate_g = [gbuf[:, i * GS:(i + 1) * GS] for i in range(NGB)]
        prod = gate_g[0]
        win_raw, wout_raw = gate_g[1][:, 0:NB * P], gate_g[1][:, NB * P:2 * NB * P]
        ids = gate_g[2][:, 0:1024].bitcast(I32)
        gws = gate_g[2][:, 1024:2048]
        MR = 6
        mask_ring = [gate_g[2][:, 2048:3072], gate_g[2][:, 3072:4096]] + \
            [gate_g[0][:, 1024 * i:1024 * i + 1024] for i in range(4)]
        mask = [mask_ring[e % MR] for e in range(E)]
        tbuf = sb("tbuf", [P, H // 2 * L])
        toep = tbuf[:, :].rearrange("p (c v) -> p c v", c=PC)
        hid = [tbuf[:, 512 * i:512 * i + 512] for i in range(FB)]
        turn = [tbuf[:, 2048 + 512 * i:2560 + 512 * i] for i in range(FB)]
        xs = sb("xs", [P, T])
        scr = sb("scr", [P, 7168])
        xrev = scr[:, 0:2048]
        gsum = scr[:, 2048:4096]
        y_gelu = scr[:, 4096:6144]
        w1_raw = scr[:, 6144:6656]
        w2_raw = scr[:, 6656:7168]
        gated = [scr[:, 512 * i:512 * i + 512] for i in range(RING)]
        whole = [scr[:, 2560 + 512 * i:3072 + 512 * i] for i in range(2)]
        o_sb = scr[:, 6144:6656]
        y_sb = scr[:, 6656:7168]
        y_t = [scr[:, 4096 + 512 * i:4608 + 512 * i] for i in range(2)]
        fin = [scr[:, 5120:5632], y_t[0]]
        xt_h, xt_l = sb("xt_h", [P, T], F32R), sb("xt_l", [P, T], F32R)
        win_h, win_l = sb("win_h", [P, NB * P], F32R), sb("win_l", [P, NB * P], F32R)
        wout_h, wout_l = sb("wout_h", [P, NB * P], F32R), sb("wout_l", [P, NB * P], F32R)
        w1_h, w1_l = sb("w1_h", [P, F], F32R), sb("w1_l", [P, F], F32R)
        w2_h, w2_l = sb("w2_h", [P, F], F32R), sb("w2_l", [P, F], F32R)
        hb_h, hb_l = sb("hb_h", [P, RING, GT], F32R), sb("hb_l", [P, RING, GT], F32R)
        x2_h, x2_l = sb("x2_h", [P, GT], F32R), sb("x2_l", [P, GT], F32R)
        AR = 3
        act_h, act_l = sb("act_h", [P, AR, GT], F32R), sb("act_l", [P, AR, GT], F32R)
        ones = sb("ones", [P, P])
        ident = sb("ident", [P, P])
        pairs = sb("pairs", [P, 32])
        nhalf = sb("nhalf", [P, TG])
        warm = sb("warm", [P, 1])
        kp = sb("kp", [P, 2 * L])
        kt = sb("kt", [L, P])
        fc = sb("fc", [P, 4 * FB + 1])
        s4 = sb("s4", [P, 4 * N + 2])
        ar, ai, cr, ci = (s4[:, N * i:N * i + N] for i in range(4))
        ldt, dsk = s4[:, 4 * N:4 * N + 1], s4[:, 4 * N + 1:4 * N + 2]
        NA = N + FB
        ang, kturn, rest, sn, sh, cs, tq = (sb(n, [P, NA]) for n in ("ang", "kturn", "rest", "sn", "sh", "cs", "tq"))
        dt_ = sb("dt_", [P, 1])
        ea, dre, mag, zm, are, den, inv, t0, t1, t2, t3 = (
            sb(n, [P, N]) for n in ("ea", "dre", "mag", "zm", "are", "den", "inv", "t0", "t1", "t2", "t3"))
        qpow = sb("qpow", [P, 8 * 2 * N])
        ppow = sb("ppow", [P, 8 * 2 * N])
        xn2 = [scr[:, 3584:4096], scr[:, 5632:6144], ppow[:, :]]
        zhi = sb("zhi", [P, 3 * 2 * N])
        td = sb("td", [P, 3 * 2 * N])
        te = sb("te", [P, 3 * 2 * N])
        tp = sb("tp", [P, 4 * 2 * N])
        tr = sb("tr", [P, 4 * 2 * N])
        cff, tbias = sb("cff", [P, FB]), sb("tbias", [P, FB])
        stat = [sb(f"stat{i}", [P, TG, 6]) for i in range(3)]
        mv = [sb(f"mv{i}", [P, TG, 2]) for i in range(3)]
        ve, rs, nmean, shift = ([sb(f"{n}{i}", [P, TG]) for i in range(4)] for n in ("ve", "rs", "nmean", "shift"))

        bank = ctx.enter_context(nc.psum_tensor("bank", [P, 8, 512], F32))
        o_ps, y_ps = bank[:, 0, :], bank[:, 3, :]
        HR = 3
        h_ps = [bank[:, 4 + i, :] for i in range(HR)]

        def f_ps(m):
            return h_ps[m % FB - 2] if m >= FB * G - 2 else bank[:, 1 + m % 2, :]

        t_ps = bank[:, 7, :]
        head_ps = [t_ps, h_ps[2]]

        names = (
            "par ffn ids gws xrev x win wout w1 w2 kpad ystore gstore "
            "nhalf cst kzero exp dre mag rest sin zm zhi inv den qpow pp pq red kp kturn kt dchain pchain "
            "whi wlo mask gsum gev conv gelu "
            "hyturn hz hvar hpower hxn hxt hxth hxtl "
            "yturn z1 stats1 var1 rstd1 xn1 xt xth xtl "
            "in gated hi lo out "
            "oev ot z2 stats2 var2 rstd2 xn2 x2t x2h x2l "
            "fin turn whole fev frac sine mix ah ahp al fout "
            "yev yt z3 stats3 var3 rstd3 res resd")
        S = {n: sem("s_" + n) for n in names.split()}
        s_toep = [[sem(f"s_toep{c}_{r}") for r in range(2)] for c in range(PC)]
        s_gate = [[sem(f"s_gate{g}_{i}") for i in range(2)] for g in range(G)]
        s_store = [sem(f"s_store{i}") for i in range(2)]
        s_yhalf = [sem(f"s_yhalf{i}") for i in range(2)]
        s_yload = [sem(f"s_yload{g}") for g in range(G)]
        s_stats = [S["stats1"], S["stats2"], S["stats3"]]
        s_power = [sem(f"s_power{k + 1}") for k in range(3)]
        s_var, s_rstd = [S["var1"], S["var2"], S["var3"]], [S["rstd1"], S["rstd2"], S["rstd3"]]

        def half(t, i):
            return t[:, i * TH * P:(i + 1) * TH * P]

        def grp(t, g):
            return t[:, g * GT:(g + 1) * GT]

        def nth(k, g):
            return g + 1 if k else g

        def own(k, g):
            return k + (g % 2 if k == 2 else 0)

        def slot(stage, g, f=0):
            t = LATE.get(g, {}).get(stage, NB * g + SLOTS[stage])
            return t + F_STEP[g] * f if stage in PER_BLOCK else t

        def due(stage, t):
            for g in range(G):
                if stage in PER_BLOCK:
                    for f in range(FB):
                        if slot(stage, g, f) == t:
                            return FB * g + f
                elif slot(stage, g) == t and (g > 0 or SLOTS[stage] > 0):
                    return g
            return None

        LAST_SLOT = slot("norm3", G - 1)
        TB = 11
        TE = 14
        ROUND_DVE = (8, 9, 10, 12, 13, 14, 15)

        turn_read = {"y_turn": S["z1"], "xt_turn": S["xtl"], "o_turn": S["z2"], "x2_turn": S["x2l"],
                     "out_turn": S["z3"]}
        turns = [(stage, g) for t in range(LAST_SLOT + 1) for stage in turn_read
                 if (g := due(stage, t)) is not None]

        block = ctx.enter_context(nc.Block())

        @block.sync
        def _(sp):
            sp.dma_start(s4[:, :], s4d_par).then_inc(S["par"], 16)
            sp.dma_start(fc[:, :], ffn_par).then_inc(S["ffn"], 16)
            sp.wait_ge(S["kzero"], 1)
            sp.dma_start(bass.AP(kpad.tensor, 0, [[2 * L * HQ, 2 * PC], [L, HQ], [1, L]]), kp[:, 0:L]) \
                .then_inc(S["kpad"], 16)
            sp.dma_start(ids, gate_id).then_inc(S["ids"], 16)
            sp.dma_start(gws, gate_w).then_inc(S["gws"], 16)
            sp.dma_start(win_raw, w_in).then_inc(S["win"], 16)
            sp.dma_start(wout_raw, w_out).then_inc(S["wout"], 16)
            sp.dma_start(xrev, x_rev).then_inc(S["xrev"], 16)
            sp.dma_start(w1_raw, w1).then_inc(S["w1"], 16)
            sp.dma_start(w2_raw, w2).then_inc(S["w2"], 16)
            sp.dma_start(xs[:, :], x).then_inc(S["x"], 16)
            sp.wait_ge(S["kt"], 1)
            sp.dma_start(bass.AP(kpad.tensor, L * HQ, [[HQ, L], [2 * L * HQ, 2 * PC], [1, HQ]]),
                         kt[:, :].rearrange("l (q h) -> l q h", h=HQ)).then_inc(S["kpad"], 16)
            sp.wait_ge(S["kpad"], 32)
            for c in range(PC):
                for r in range(2):
                    sp.dma_start(toep[L * r:L * r + L, c, :],
                                 bass.AP(kpad.tensor, (PC * r + c) * 2 * L * HQ + HQ, [[HQ, L], [1, L * HQ]])) \
                        .then_inc(s_toep[c][r], 16)
            def store_gates(a):
                sp.wait_ge(S["gev"], a + 1)
                for q in range(2):
                    sp.dma_start(bass.AP(gates.tensor, 4 * a * T + T // 2 * q, [[T, 4], [1, T // 2]]),
                                 gsum[q:P:32, T // 2 * a:T // 2 * (a + 1)]).then_inc(S["gstore"], 16)

            store_gates(0)
            for c in range(2):
                for r in range(2):
                    sp.wait_ge(S["gelu"], 2 * c + r + 1)
                    o = (HH * r + HH // 2 * c) * L
                    sp.dma_start(bass.AP(y_dram.tensor, o, [[2 * HH * L, JC], [H * L, B], [1, HH // 2 * L]]),
                                 y_gelu[:, o:o + HH // 2 * L]).then_inc(S["ystore"], 16)

            def load_gates(g, i):
                if g >= NGB:
                    sp.wait_ge(S["gated"], NB * (g - NGB + 1))
                EH = E // 2
                sp.dma_start(gate_g[g % NGB][:, i * EH * GT:(i + 1) * EH * GT]
                             .rearrange("p (e t) -> p e t", e=EH),
                             bass.AP(gates.tensor, i * EH * T + g * GT, [[0, P], [T, EH], [1, GT]])) \
                    .then_inc(s_gate[g][i], 16)

            def load_y(g):
                if g == 2:
                    sp.wait_ge(S["hyturn"], 2)
                elif g > 2:
                    sp.wait_ge(S["yturn"], g - 2)
                sp.dma_start(y_t[g % 2].rearrange("h (b l) -> h b l", l=L),
                             bass.AP(y_dram.tensor, g * BG * H * L, [[L, H], [H * L, BG], [1, L]])) \
                    .then_inc(s_yload[g], 16)

            sp.wait_ge(S["ystore"], 16 * 4)
            for i in range(2):
                sp.dma_start(half(y_t[0], i).rearrange("h (b l) -> h b l", l=L),
                             bass.AP(y_dram.tensor, i * BG // 2 * H * L, [[L, H], [H * L, BG // 2], [1, L]])) \
                    .then_inc(s_yhalf[i], 16)
            store_gates(1)
            sp.wait_ge(S["gstore"], 64)
            load_gates(0, 0)
            load_y(1)
            load_gates(0, 1)
            sp.wait_ge(S["wlo"], 10)
            load_gates(1, 0)
            load_gates(1, 1)
            load_y(2)
            load_gates(2, 0)
            load_gates(2, 1)
            load_y(3)
            load_gates(3, 0)
            load_gates(3, 1)
            for g in range(G):
                sp.wait_ge(S["res"], g + 1)
                if g == G - 1:
                    sp.wait_ge(S["resd"], 1)
                sp.dma_start(grp(out, g), fin[g % 2]).then_inc(s_store[g % 2], 16)
            for i in range(2):
                sp.wait_ge(s_store[i], 16 * G // 2)

        @block.gpsimd
        def _(pool):
            chain = [0]

            def link(ins):
                chain[0] += 1
                ins.then_inc(S["pchain"], 1)
                pool.wait_ge(S["pchain"], chain[0])

            tt = nc.gpsimd.tensor_tensor
            nc.gpsimd.memset(nhalf[:, :], -0.5).then_inc(S["nhalf"], 1)
            nc.gpsimd.memset(pairs[:, :], 0.0).then_inc(S["cst"], 1)
            link(nc.gpsimd.memset(ones[:, :], 1.0))
            pool.wait_ge(S["cst"], 1)
            nc.gpsimd.affine_select(out=ident[:, :], in_=ones[:, :], compare_op=ALU.is_equal, fill=0.0,
                                    base=0, pattern=[[-1, P]], channel_multiplier=1).then_inc(S["cst"], 1)
            pool.wait_ge(S["cst"], 2)
            for q in range(2):
                nc.gpsimd.memset(pairs[L * q:L * q + L, q:q + 1], 1.0).then_inc(S["cst"], 1)
                pool.wait_ge(S["cst"], 3 + q)

            pool.wait_ge(S["par"], 16)
            pool.wait_ge(S["exp"], 1)
            nc.gpsimd.tensor_scalar(are[:, :], ea[:, :], -1.0, None, ALU.mult)
            tt(t0[:, :], ea[:, :], ea[:, :], ALU.mult)
            link(tt(t1[:, :], ai, ai, ALU.mult))
            link(tt(den[:, :], t0[:, :], t1[:, :], ALU.add))
            nc.gpsimd.tensor_scalar(den[:, :], den[:, :], 0.5, None, ALU.mult).then_inc(S["den"], 1)
            tt(t0[:, :], cr, are[:, :], ALU.mult)
            tt(t1[:, :], ci, ai, ALU.mult)
            tt(t2[:, :], ci, are[:, :], ALU.mult)
            link(tt(t3[:, :], cr, ai, ALU.mult))
            nri = tp[:, 0:2 * N]
            tt(nri[:, 0:N], t0[:, :], t1[:, :], ALU.add)
            link(tt(nri[:, N:2 * N], t2[:, :], t3[:, :], ALU.subtract))
            pool.wait_ge(S["inv"], 1)
            pair = [[N, 2], [1, N]]
            link(tt(view(nri, pair), view(nri, pair), view(inv[:, :], [[0, 2], [1, N]]), ALU.mult))
            pool.wait_ge(S["zm"], 1)
            zc = qpow[:, 3 * N:4 * N]
            nz, nc_ = tr[:, 0:2 * N], tr[:, 2 * N:4 * N]
            tt(view(nz, pair), view(nri, pair), view(zm[:, :], [[0, 2], [1, N]]), ALU.mult)
            link(tt(view(nc_, pair), view(nri, pair), view(zc, [[0, 2], [1, N]]), ALU.mult))
            tt(ppow[:, 0:N], nz[:, 0:N], nc_[:, N:2 * N], ALU.add)
            link(tt(ppow[:, N:2 * N], nz[:, N:2 * N], nc_[:, 0:N], ALU.subtract))
            for i, m in enumerate((1, 2, 4)):
                pool.wait_ge(S["zhi"], i + 1)
                src = ppow[:, 0:2 * N * m]
                yr = zhi[:, 2 * N * i:2 * N * i + N]
                yc = zhi[:, 2 * N * i + N:2 * N * i + 2 * N]
                s3 = [[2 * N, m], [N, 2], [1, N]]
                tt(view(tp[:, :], s3), view(src, s3), view(yr, [[0, m], [0, 2], [1, N]]), ALU.mult)
                link(tt(view(tr[:, :], s3), view(src, s3), view(yc, [[0, m], [0, 2], [1, N]]), ALU.mult))
                dst = ppow[:, 2 * N * m:4 * N * m]
                s2 = [[2 * N, m], [1, N]]
                tt(view(dst, s2), view(tp[:, :], s2), view(tr[:, :], s2, N), ALU.add)
                tt(view(dst, s2, N), view(tp[:, :], s2, N), view(tr[:, :], s2), ALU.subtract).then_inc(S["pp"], 1)
                pool.wait_ge(S["pp"], i + 1)
            pool.wait_ge(S["qpow"], 1)
            share = prod[:, 6 * 16 * N:8 * 16 * N]
            link(tt(view(share, [[16 * N, 2], [2 * N, 8], [1, 2 * N]]),
                    view(ppow[:, :], [[2 * N, 2], [0, 8], [1, 2 * N]], 12 * N),
                    view(qpow[:, :], [[0, 2], [2 * N, 8], [1, 2 * N]]), ALU.mult))
            tt(view(share, [[2 * N, 16], [1, N]]), view(share, [[2 * N, 16], [1, N]]),
               view(share, [[2 * N, 16], [1, N]], N), ALU.add).then_inc(S["pq"], 1)

            for i, (dst, raw, high, cols) in enumerate((
                    (win_l, win_raw, win_h, NB * P), (wout_l, wout_raw, wout_h, NB * P),
                    (w1_l, w1_raw, w1_h, F), (w2_l, w2_raw, w2_h, F))):
                pool.wait_ge(S["whi"], i + 1)
                for o in range(0, cols, 512):
                    w = slice(o, o + 512)
                    tt(dst[:, w], raw[:, w], high[:, w].bitcast(F32), ALU.subtract).then_inc(S["wlo"], 1)

            def inv_std(k, g):
                pool.wait_ge(s_var[k], nth(k, g))
                o = own(k, g)
                if k == 2 and g >= 2:
                    pool.wait_ge(S["res"], g - 1)
                tt(rs[o][:, :], ve[o][:, :], nhalf[:, :], ALU.pow).then_inc(s_power[k], 1)
                if k != 1:
                    pool.wait_ge(s_power[k], nth(k, g))
                    tt(shift[o][:, :], nmean[o][:, :], rs[o][:, :], ALU.mult).then_inc(s_rstd[k], 1)

            def low(n):
                pool.wait_ge(S["hi"], n + 1)
                if n >= RING:
                    pool.wait_ge(S["out"], n - RING + 1)
                tt(hb_l[:, n % RING, :], gated[n % RING], hb_h[:, n % RING, :].bitcast(F32), ALU.subtract) \
                    .then_inc(S["lo"], 1)

            for i in range(2):
                pool.wait_ge(S["hvar"], i + 1)
                tt(rs[0][:, TH * i:TH * i + TH], ve[0][:, TH * i:TH * i + TH], nhalf[:, 0:TH], ALU.pow) \
                    .then_inc(S["hpower"], 1)
            for t in range(LAST_SLOT + 1):
                for k in range(3):
                    g = due(f"rstd{k + 1}", t)
                    if g is not None:
                        inv_std(k, g)
                if t < NB * G:
                    low(t)
                if (m := due("f_high", t)) is not None and TB <= m < TE:
                    pool.wait_ge(S["mix"], m + 1)
                    pool.wait_ge(S["fout"], m - AR + 1)
                    nc.gpsimd.tensor_scalar(act_h[:, m % AR, :], hid[m % FB], 0.0, None, ALU.max) \
                        .then_inc(S["ahp"], 1)

        @block.scalar
        def _(act):
            av = nc.scalar.activation
            act.wait_ge(S["nhalf"], 1)
            av(warm[:, :], nhalf[:, 0:1], ACT.Exp)
            act.wait_ge(S["par"], 16)
            av(dt_[:, :], ldt, ACT.Exp)
            av(ea[:, :], ar, ACT.Exp).then_inc(S["exp"], 1)
            act.wait_ge(S["dre"], 1)
            av(mag[:, :], dre[:, :], ACT.Exp).then_inc(S["mag"], 1)
            act.wait_ge(S["rest"], 1)
            av(sn[:, :], rest[:, :], ACT.Sin)
            av(sh[:, :], rest[:, :], ACT.Sin, scale=0.5).then_inc(S["sin"], 1)
            for arrived, dst, raw in (("win", win_h, win_raw), ("wout", wout_h, wout_raw), ("w1", w1_h, w1_raw),
                                      ("w2", w2_h, w2_raw)):
                act.wait_ge(S[arrived], 16)
                av(dst[:, :], raw, ACT.Copy).then_inc(S["whi"], 1)
            act.wait_ge(S["kturn"], 1)
            av(kt[:, :], bank[0:L, 0, 0:P], ACT.Copy).then_inc(S["kt"], 1)

            def gate_rows(a):
                act.wait_ge(S["gsum"], 8 * (a + 1))
                av(gsum[:, 1024 * a:1024 * a + 1024], bank[:, 4 + 2 * a:6 + 2 * a, :].rearrange("p a b -> p (a b)"),
                   ACT.Copy).then_inc(S["gev"], 1)

            gate_rows(0)
            for c in range(2):
                act.wait_ge(S["conv"], PC // 2 * (c + 1))
                for r in range(2):
                    o = (2 * r + c) * GT
                    av(y_gelu[:, o:o + GT], bank[:, 2 * c + r, :], ACT.Gelu).then_inc(S["gelu"], 1)
            gate_rows(1)

            def normalise(buf, k, g, done, tiles=range(TG)):
                act.wait_ge(s_rstd[k], nth(k, g))
                for c in tiles:
                    last = av(buf[:, c * P:(c + 1) * P], buf[:, c * P:(c + 1) * P], ACT.Identity,
                              bias=shift[own(k, g)][:, c:c + 1], scale=rs[own(k, g)][:, c:c + 1])
                last.then_inc(done, 1)

            def xt_high(g):
                act.wait_ge(S["xt"], g)
                av(grp(xt_h, g), t_ps, ACT.Copy).then_inc(S["xth"], 1)

            for i in range(2):
                act.wait_ge(S["hxt"], i + 1)
                av(half(xt_h, i), half(head_ps[i], i), ACT.Copy).then_inc(S["hxth"], 1)

            def high(n):
                act.wait_ge(S["gated"], n + 1)
                if n >= RING:
                    act.wait_ge(S["out"], n - RING + 1)
                av(hb_h[:, n % RING, :], gated[n % RING], ACT.Copy).then_inc(S["hi"], 1)

            def f_turn(m):
                f = m % FB
                act.wait_ge(S["fin"], m + 1)
                if m >= FB:
                    act.wait_ge(S["al"], m - FB + 1)
                av(turn[f], f_ps(m), ACT.Identity, bias=tbias[:, f:f + 1], scale=0.1 * INV_TWO_PI) \
                    .then_inc(S["turn"], 1)
                if m in ROUND_DVE:
                    return
                act.wait_ge(S["turn"], m + 1)
                if m >= 2:
                    act.wait_ge(S["frac"], m - 1)
                av(whole[m % 2], turn[f], ACT.Copy, bias=ROUND).then_inc(S["whole"], 1)

            def f_hid(m):
                f = m % FB
                av(hid[f], f_ps(m), ACT.Identity, bias=fc[:, 3 * FB + f:3 * FB + f + 1]).then_inc(S["fev"], 1)

            def f_sine(m):
                act.wait_ge(S["frac"], m + 1)
                av(turn[m % FB], turn[m % FB], ACT.Sin, scale=-TWO_PI_BELOW).then_inc(S["sine"], 1)

            def f_high(m):
                act.wait_ge(S["mix"], m + 1)
                if m >= AR:
                    act.wait_ge(S["fout"], m - AR + 1)
                av(act_h[:, m % AR, :], hid[m % FB], ACT.Relu).then_inc(S["ah"], 1)

            for t in range(LAST_SLOT + 1):
                if (g := due("o_evac", t)) is not None:
                    act.wait_ge(S["out"], NB * (g + 1))
                    if g >= 1:
                        act.wait_ge(S["ot"], g)
                    av(o_sb, o_ps, ACT.Copy).then_inc(S["oev"], 1)
                if t < NB * G:
                    high(t)
                for stage, tiles in (("norm1a", range(TG // 2)), ("norm1b", range(TG // 2, TG))):
                    if (g := due(stage, t)) is not None:
                        normalise(grp(xs, g), 0, g, S["xn1"], tiles)
                if (g := due("xt_high", t)) is not None:
                    xt_high(g)
                if (g := due("x2_high", t)) is not None:
                    act.wait_ge(S["x2t"], g + 1)
                    if g >= 1:
                        act.wait_ge(S["fin"], FB * g)
                    av(x2_h[:, :], t_ps, ACT.Copy).then_inc(S["x2h"], 1)
                if (m := due("f_high", t)) is not None and not TB <= m < TE:
                    f_high(m)
                if (m := due("f_sine", t)) is not None:
                    f_sine(m)
                if (m := due("f_hid", t)) is not None:
                    f_hid(m)
                if (m := due("f_turn", t)) is not None:
                    f_turn(m)
                if (g := due("y_evac", t)) is not None:
                    act.wait_ge(S["fout"], FB * (g + 1))
                    if g >= 1:
                        act.wait_ge(S["yt"], g)
                    av(y_sb, y_ps, ACT.Identity, bias=fc[:, 4 * FB:4 * FB + 1]).then_inc(S["yev"], 1)
                if (g := due("norm3", t)) is not None:
                    normalise(fin[g % 2], 2, g, S["res"], range(TG if g < G - 1 else TG // 2))

        @block.vector
        def _(dve):
            chain = [0]

            def link(ins):
                chain[0] += 1
                ins.then_inc(S["dchain"], 1)
                dve.wait_ge(S["dchain"], chain[0])

            tt, ts, stt = nc.vector.tensor_tensor, nc.vector.tensor_scalar, nc.vector.scalar_tensor_tensor
            nc.vector.memset(kp[:, 0:L], 0.0).then_inc(S["kzero"], 1)
            nc.vector.memset(qpow[:, 0:N], 1.0)
            link(nc.vector.memset(qpow[:, N:2 * N], 0.0))
            dve.wait_ge(S["par"], 16)
            dve.wait_ge(S["ffn"], 16)
            nc.vector.tensor_copy(ang[:, N:NA], fc[:, 0:FB])
            dve.wait_ge(S["exp"], 1)
            ts(dre[:, :], ea[:, :], dt_[:, 0:1], -1.0, ALU.mult, ALU.mult).then_inc(S["dre"], 1)
            link(ts(ang[:, 0:N], ai, dt_[:, 0:1], None, ALU.mult))
            link(ts(kturn[:, :], ang[:, :], INV_TWO_PI, ROUND, ALU.mult, ALU.add))
            link(ts(kturn[:, :], kturn[:, :], ROUND, None, ALU.subtract))
            link(stt(rest[:, :], kturn[:, :], -TWO_PI_HI, ang[:, :], ALU.mult, ALU.add))
            link(stt(rest[:, :], kturn[:, :], -TWO_PI_LO, rest[:, :], ALU.mult, ALU.add))
            ts(rest[:, :], rest[:, :], PI_BELOW, -PI_BELOW, ALU.min, ALU.max).then_inc(S["rest"], 1)
            dve.wait_ge(S["den"], 1)
            nc.vector.reciprocal(inv[:, :], den[:, :]).then_inc(S["inv"], 1)
            dve.wait_ge(S["sin"], 1)
            link(tt(cs[:, :], sh[:, :], sh[:, :], ALU.mult))
            link(ts(cs[:, :], cs[:, :], -2.0, 1.0, ALU.mult, ALU.add))
            dve.wait_ge(S["mag"], 1)
            z1 = qpow[:, 2 * N:4 * N]
            tt(z1[:, 0:N], mag[:, :], cs[:, 0:N], ALU.mult)
            link(stt(z1[:, N:2 * N], mag[:, :], -1.0, sn[:, 0:N], ALU.mult, ALU.mult))
            ts(zm[:, :], z1[:, 0:N], -1.0, None, ALU.add).then_inc(S["zm"], 1)

            def square(dst, src):
                tt(td[:, 0:2 * N], src, src, ALU.mult)
                link(stt(dst[:, N:2 * N], src[:, 0:N], 2.0, src[:, N:2 * N], ALU.mult, ALU.mult))
                return tt(dst[:, 0:N], td[:, 0:N], td[:, N:2 * N], ALU.subtract)

            def times(dst, src, by, m):
                s3 = [[2 * N, m], [N, 2], [1, N]]
                tt(view(td[:, :], s3), view(src, s3), view(by[:, 0:N], [[0, m], [0, 2], [1, N]]), ALU.mult)
                link(tt(view(te[:, :], s3), view(src, s3), view(by[:, N:2 * N], [[0, m], [0, 2], [1, N]]), ALU.mult))
                s2 = [[2 * N, m], [1, N]]
                tt(view(dst, s2), view(td[:, :], s2), view(te[:, :], s2, N), ALU.subtract)
                return tt(view(dst, s2, N), view(td[:, :], s2, N), view(te[:, :], s2), ALU.add)

            def q_(c, m=1):
                return qpow[:, 2 * N * c:2 * N * (c + m)]

            link(square(q_(2), q_(1)))
            link(square(q_(4), q_(2)))
            for i in range(3):
                square(zhi[:, 2 * N * i:2 * N * (i + 1)], q_(4) if i == 0 else zhi[:, 2 * N * (i - 1):2 * N * i]) \
                    .then_inc(S["zhi"], 1)
                dve.wait_ge(S["zhi"], i + 1)
            link(times(q_(3), q_(2), q_(1), 1))
            times(q_(5, 3), q_(1, 3), q_(4), 3).then_inc(S["qpow"], 1)
            dve.wait_ge(S["qpow"], 1)
            for a, m, need in ((0, 4, 2), (4, 2, 3)):
                dve.wait_ge(S["pp"], need)
                part = prod[:, 16 * N * a:16 * N * (a + m)]
                link(tt(view(part, [[16 * N, m], [2 * N, 8], [1, 2 * N]]),
                        view(ppow[:, :], [[2 * N, m], [0, 8], [1, 2 * N]], 2 * N * a),
                        view(qpow[:, :], [[0, m], [2 * N, 8], [1, 2 * N]]), ALU.mult))
                nc.vector.tensor_reduce(kp[:, L + 8 * a:L + 8 * (a + m)], part.rearrange("p (l n) -> p l n", n=2 * N),
                                        AX_X, ALU.add)
            dve.wait_ge(S["pq"], 1)
            nc.vector.tensor_reduce(kp[:, L + 48:L + 64], view(prod[:, 6 * 16 * N:8 * 16 * N], [[2 * N, 16], [1, N]]),
                                    AX_X, ALU.add).then_inc(S["red"], 1)
            dve.wait_ge(S["red"], 1)
            ts(kp[:, L:L + 1], kp[:, L:L + 1], dsk, None, ALU.add).then_inc(S["kp"], 1)

            tt(tq[:, 0:FB], cs[:, N:NA], fc[:, FB:2 * FB], ALU.mult)
            link(tt(kturn[:, 0:FB], sn[:, N:NA], fc[:, 2 * FB:3 * FB], ALU.mult))
            link(tt(tq[:, 0:FB], tq[:, 0:FB], kturn[:, 0:FB], ALU.add))
            stt(cff[:, :], tq[:, 0:FB], 0.1, fc[:, 2 * FB:3 * FB], ALU.mult, ALU.mult)
            link(ts(tbias[:, :], rest[:, N:NA], INV_TWO_PI, None, ALU.mult))
            link(stt(tbias[:, :], fc[:, 3 * FB:4 * FB], 0.1 * INV_TWO_PI, tbias[:, :], ALU.mult, ALU.add))

            dve.wait_ge(S["ids"], 16)
            dve.wait_ge(S["gws"], 16)
            for e in range(E):
                if e >= MR:
                    dve.wait_ge(S["gsum"], 2 * (e - MR + 1))
                stt(mask[e], ids, float(e), gws, ALU.is_equal, ALU.mult).then_inc(S["mask"], 1)

            def stats(src, k):
                for c in range(TG):
                    last = nc.vector.bn_stats(stat[k][:, c, :], src[:, c * P:(c + 1) * P])
                last.then_inc(s_stats[k], 1)

            def variance(k, g):
                dve.wait_ge(s_stats[k], nth(k, g))
                for c in range(TG):
                    last = nc.vector.bn_aggr(mv[k][:, c, :], stat[k][:, c, :])
                link(last)
                o = own(k, g)
                if k != 1:
                    if nth(k, g) >= 2:
                        dve.wait_ge(s_rstd[k], nth(k, g) - 1)
                    ts(nmean[o][:, :], view(mv[k][:, 0, :], [[2, TG]]), -1.0, None, ALU.mult)
                ts(ve[o][:, :], view(mv[k][:, 0, :], [[2, TG]], 1), EPS, None, ALU.add).then_inc(s_var[k], 1)

            def normalise(buf, k, g, done, tiles=range(TG)):
                dve.wait_ge(s_power[k], g + 1)
                for c in tiles:
                    last = ts(buf[:, c * P:(c + 1) * P], buf[:, c * P:(c + 1) * P], mv[k][:, c, 0:1],
                              rs[own(k, g)][:, c:c + 1], ALU.subtract, ALU.mult)
                last.then_inc(done, 1)

            def add_gelu(g):
                dve.wait_ge(S["yturn"], g)
                tt(grp(xs, g), t_ps, grp(xs, g), ALU.add).then_inc(S["z1"], 1)

            def xt_low(g):
                dve.wait_ge(S["xth"], g)
                tt(grp(xt_l, g), t_ps, grp(xt_h, g).bitcast(F32), ALU.subtract).then_inc(S["xtl"], 1)

            dve.wait_ge(S["x"], 16)
            for i in range(2):
                tiles = range(TH * i, TH * i + TH)
                dve.wait_ge(S["hyturn"], i + 1)
                tt(half(xs, i), half(head_ps[i], i), half(xs, i), ALU.add).then_inc(S["hz"], 1)
                dve.wait_ge(S["hz"], i + 1)
                for c in tiles:
                    last = nc.vector.bn_stats(stat[0][:, c, :], xs[:, c * P:(c + 1) * P])
                link(last)
                for c in tiles:
                    last = nc.vector.bn_aggr(mv[0][:, c, :], stat[0][:, c, :])
                link(last)
                ts(ve[0][:, TH * i:TH * i + TH], view(mv[0][:, TH * i, :], [[2, TH]], 1), EPS, None, ALU.add) \
                    .then_inc(S["hvar"], 1)
            for i in range(2):
                dve.wait_ge(S["hpower"], i + 1)
                for c in range(TH * i, TH * i + TH):
                    last = ts(xs[:, c * P:(c + 1) * P], xs[:, c * P:(c + 1) * P], mv[0][:, c, 0:1], rs[0][:, c:c + 1],
                              ALU.subtract, ALU.mult)
                last.then_inc(S["hxn"], 1)
            for i in range(2):
                dve.wait_ge(S["hxth"], i + 1)
                tt(half(xt_l, i), half(head_ps[i], i), half(xt_h, i).bitcast(F32), ALU.subtract).then_inc(S["hxtl"], 1)

            def gate_block(n):
                g, j = divmod(n, NB)
                if j % (NB // 2) == 0:
                    dve.wait_ge(s_gate[g][j // (NB // 2)], 16)
                dve.wait_ge(S["in"], n + 1)
                if n >= RING:
                    dve.wait_ge(S["hi"], n - RING + 1)
                    dve.wait_ge(S["lo"], n - RING + 1)
                e = j // DH
                stt(gated[n % RING], h_ps[n % HR], 0.0, gate_g[g % NGB][:, e * GT:(e + 1) * GT],
                    ALU.max, ALU.mult).then_inc(S["gated"], 1)

            def f_frac(m):
                if m not in ROUND_DVE:
                    dve.wait_ge(S["whole"], sum(k not in ROUND_DVE for k in range(m + 1)))
                else:
                    dve.wait_ge(S["turn"], m + 1)
                    link(ts(whole[m % 2], turn[m % FB], ROUND, None, ALU.add))
                stt(turn[m % FB], whole[m % 2], ROUND, turn[m % FB], ALU.subtract, ALU.subtract) \
                    .then_inc(S["frac"], 1)

            def f_mix(m):
                f = m % FB
                dve.wait_ge(S["sine"], m + 1)
                stt(hid[f], turn[f], cff[:, f:f + 1], hid[f], ALU.mult, ALU.add).then_inc(S["mix"], 1)

            def f_low(m):
                if TB <= m < TE:
                    dve.wait_ge(S["ahp"], m + 1 - TB)
                else:
                    dve.wait_ge(S["ah"], m + 1 if m < TB else m + 1 - (TE - TB))
                if m >= AR:
                    dve.wait_ge(S["fout"], m - AR + 1)
                stt(act_l[:, m % AR, :], hid[m % FB], 0.0, act_h[:, m % AR, :].bitcast(F32),
                    ALU.max, ALU.subtract).then_inc(S["al"], 1)

            for t in range(LAST_SLOT + 1):
                if t < NB * G:
                    gate_block(t)
                if (g := due("z1", t)) is not None:
                    add_gelu(g)
                if (g := due("xt_low", t)) is not None:
                    xt_low(g)
                if (g := due("z2", t)) is not None:
                    dve.wait_ge(S["ot"], g + 1)
                    tt(xn2[g % 3], t_ps, grp(xs, g), ALU.add).then_inc(S["z2"], 1)
                for k, z, src in ((0, "z1", lambda g: grp(xs, g)), (1, "z2", lambda g: xn2[g % 3]),
                                  (2, "z3", lambda g: fin[g % 2])):
                    if (g := due(f"stats{k + 1}", t)) is not None:
                        dve.wait_ge(S[z], nth(k, g))
                        stats(src(g), k)
                    if (g := due(f"var{k + 1}", t)) is not None:
                        variance(k, g)
                if (g := due("norm2", t)) is not None:
                    normalise(xn2[g % 3], 1, g, S["xn2"])
                if (g := due("x2_low", t)) is not None:
                    dve.wait_ge(S["x2h"], g + 1)
                    if g >= 1:
                        dve.wait_ge(S["fin"], FB * g)
                    tt(x2_l[:, :], t_ps, x2_h[:, :].bitcast(F32), ALU.subtract).then_inc(S["x2l"], 1)
                if (m := due("f_low", t)) is not None:
                    f_low(m)
                if (m := due("f_mix", t)) is not None:
                    f_mix(m)
                if (m := due("f_frac", t)) is not None:
                    f_frac(m)
                if (g := due("z3", t)) is not None:
                    dve.wait_ge(S["yt"], g + 1)
                    if g >= 2:
                        dve.wait_ge(s_store[g % 2], 16 * (g // 2))
                    tt(fin[g % 2], t_ps, xn2[g % 3], ALU.add).then_inc(S["z3"], 1)
                if due("norm3", t) == G - 1:
                    normalise(fin[(G - 1) % 2], 2, G - 1, S["resd"], range(TG // 2, TG))

        @block.tensor
        def _(pe):
            mm = nc.tensor.matmul
            pe.wait_ge(S["cst"], 4)
            pe.wait_ge(S["kp"], 1)
            nc.tensor.transpose(bank[0:L, 0, 0:P], kp[:, L:2 * L], ident[:, :]).then_inc(S["kturn"], 1)
            def gate_sums(experts):
                for e in experts:
                    pe.wait_ge(S["mask"], e + 1)
                    for i in range(2):
                        mm(bank[32 * (e % 4):32 * (e % 4) + 32, 4 + 2 * (e // 4) + i, :], pairs[:, :],
                           mask[e][:, i * 512:(i + 1) * 512], start=True, stop=True).then_inc(S["gsum"], 1)

            gate_sums(range(E // 2))
            pe.wait_ge(S["xrev"], 16)
            xr = xrev.rearrange("p (b h) -> p h b", b=B)
            for c in range(PC):
                for r in range(2):
                    pe.wait_ge(s_toep[c][r], 16)
                for i in range(HI):
                    for j in range(JC):
                        for r in range(2):
                            b, at = divmod(HI * c + i, GT // L)
                            last = mm(bank[32 * j:32 * j + 32, 2 * b + r, at * L:(at + 1) * L],
                                      xr[L * r:L * r + L, HH * j + HI * c + i, :],
                                      view(toep[L * r:L * r + L, c, :], [[HQ, L]], HI * j + i),
                                      start=True, stop=True)
                last.then_inc(S["conv"], 1)

            gate_sums(range(E // 2, E))

            def three(dst, wh, wl, vh, vl, first, last, low_ready=None):
                mm(dst, wh, vh, start=first, stop=False)
                mm(dst, wl, vh, start=False, stop=False)
                if low_ready:
                    pe.wait_ge(*low_ready)
                return mm(dst, wh, vl, start=False, stop=last)

            def turn4(dst, src, done, tiles=range(TG)):
                for c in tiles:
                    last = nc.tensor.transpose(dst[:, c * P:(c + 1) * P], src[:, c * P:(c + 1) * P], ident[:, :])
                last.then_inc(S[done], 1)

            def y_turn(g):
                pe.wait_ge(s_yload[g], 16)
                turn4(t_ps, y_t[g % 2], "yturn")

            def xt_turn(g):
                pe.wait_ge(S["xn1"], 2 * g)
                turn4(t_ps, grp(xs, g), "xt")

            pe.wait_ge(S["gev"], 2)
            for i in range(2):
                pe.wait_ge(s_yhalf[i], 16)
                turn4(head_ps[i], y_t[0], "hyturn", range(TH * i, TH * i + TH))
            for i in range(2):
                pe.wait_ge(S["hxn"], i + 1)
                turn4(head_ps[i], xs, "hxt", range(TH * i, TH * i + TH))
            pe.wait_ge(S["wlo"], 10)

            def before_read(stage, g):
                i = turns.index((stage, g))
                if i == 0:
                    pe.wait_ge(S["hxtl"], 2)
                else:
                    before, k = turns[i - 1]
                    pe.wait_ge(turn_read[before], k if before in ("y_turn", "xt_turn") else k + 1)

            def first_product(n):
                g, j = divmod(n, NB)
                if j == 0:
                    if g:
                        pe.wait_ge(S["xth"], g)
                    else:
                        pe.wait_ge(S["hxth"], 2)
                if n >= HR:
                    pe.wait_ge(S["gated"], n - HR + 1)
                w = slice(j * P, (j + 1) * P)
                three(h_ps[n % HR], win_h[:, w], win_l[:, w], grp(xt_h, g), grp(xt_l, g), True, True,
                      ((S["xtl"], g) if g else (S["hxtl"], 2)) if j == 0 else None) \
                    .then_inc(S["in"], 1)

            def second_product(n):
                g, j = divmod(n, NB)
                if n == 0:
                    pe.wait_ge(S["gelu"], 4)
                if j == 0 and g >= 1:
                    pe.wait_ge(S["oev"], g)
                pe.wait_ge(S["hi"], n + 1)
                w = slice(j * P, (j + 1) * P)
                r = n % RING
                three(o_ps, wout_h[:, w], wout_l[:, w], hb_h[:, r, :], hb_l[:, r, :], j == 0, j == NB - 1,
                      (S["lo"], n + 1)) \
                    .then_inc(S["out"], 1)

            def f_first(m):
                f = m % FB
                if f == 0:
                    pe.wait_ge(S["x2h"], m // FB + 1)
                if m >= FB * G - 2:
                    pe.wait_ge(S["gated"], NB * G)
                elif m >= 2:
                    pe.wait_ge(S["fev"], m - 1)
                w = slice(f * P, (f + 1) * P)
                three(f_ps(m), w1_h[:, w], w1_l[:, w], x2_h[:, :], x2_l[:, :], True, True,
                      (S["x2l"], m // FB + 1) if f == 0 else None) \
                    .then_inc(S["fin"], 1)

            def f_second(m):
                f = m % FB
                if f == 0 and m >= FB:
                    pe.wait_ge(S["yev"], m // FB)
                if TB <= m < TE:
                    pe.wait_ge(S["ahp"], m + 1 - TB)
                else:
                    pe.wait_ge(S["ah"], m + 1 if m < TB else m + 1 - (TE - TB))
                w = slice(f * P, (f + 1) * P)
                r = m % AR
                three(y_ps, w2_h[:, w], w2_l[:, w], act_h[:, r, :], act_l[:, r, :], f == 0, f == FB - 1,
                      (S["al"], m + 1)) \
                    .then_inc(S["fout"], 1)

            for t in range(LAST_SLOT + 1):
                if t < NB * G:
                    first_product(t)
                if LAG <= t < NB * G + LAG:
                    second_product(t - LAG)
                if (g := due("y_turn", t)) is not None:
                    before_read("y_turn", g)
                    y_turn(g)
                if (g := due("xt_turn", t)) is not None:
                    before_read("xt_turn", g)
                    xt_turn(g)
                if (g := due("o_turn", t)) is not None:
                    before_read("o_turn", g)
                    pe.wait_ge(S["oev"], g + 1)
                    turn4(t_ps, o_sb, "ot")
                if (g := due("x2_turn", t)) is not None:
                    before_read("x2_turn", g)
                    pe.wait_ge(S["xn2"], g + 1)
                    turn4(t_ps, xn2[g % 3], "x2t")
                if (g := due("out_turn", t)) is not None:
                    before_read("out_turn", g)
                    pe.wait_ge(S["yev"], g + 1)
                    turn4(t_ps, y_sb, "yt")
                if (m := due("f_first", t)) is not None:
                    f_first(m)
                if (m := due("f_second", t)) is not None:
                    f_second(m)


def kernel(**inputs):
    import numpy as _np
    import concourse.bacc as _bacc
    from concourse import mybir as _mybir
    from concourse.bass_utils import run_bass_kernel_spmd as _run

    a = {k: _np.asarray(v) for k, v in inputs.items()}
    x = a['x']
    b, l, h = x.shape
    t = b * l
    experts, d, _ = a['L0_xattn_proj_in'].shape
    f = a['L0_ffn_W1'].shape[1]

    def halves(v):
        return v.reshape(2, b // 2, l, l).transpose(0, 2, 1, 3).reshape(2 * l, t // 2)

    def blocks(v):
        return v.reshape(-1, 128).T

    laid = {
        "x": x.reshape(t // 128, 128, h).transpose(1, 0, 2).reshape(128, t),
        "x_rev": x[:, ::-1, :].reshape(b, l, 4, 2, 16).transpose(3, 1, 0, 2, 4).reshape(128, t),
        "gate_w": halves(a['ctx_512']),
        "gate_id": halves(a['itok_BxS2xS_0_7']),
        "s4d_par": _np.concatenate(
            [a['L0_attn_A_real'], a['L0_attn_A_imag'], a['L0_attn_C_real'], a['L0_attn_C_imag'],
             a['L0_attn_log_dt'].reshape(h, 1), _np.broadcast_to(a['L0_attn_D'].reshape(1, 1), (h, 1))], axis=1)
        .reshape(4, 2, 4, 4, -1).transpose(1, 2, 0, 3, 4).reshape(h, -1),
        "w_in": a['L0_xattn_proj_in'].transpose(2, 0, 1).reshape(h, experts * d),
        "w_out": a['L0_xattn_proj_out'].reshape(experts, h, d // 128, 128).transpose(3, 0, 2, 1)
        .reshape(128, experts * d),
        "w1": a['L0_ffn_W1'],
        "w2": a['L0_ffn_W2'].reshape(f // 128, 128, h).transpose(1, 0, 2).reshape(128, f),
        "ffn_par": _np.concatenate(
            [blocks(a['L0_ffn_quantum_phases']), blocks(a['L0_ffn_quantum_weights_real']),
             blocks(a['L0_ffn_quantum_weights_imag']), blocks(a['L0_ffn_b1']), blocks(a['L0_ffn_b2'])], axis=1),
    }
    nc = _bacc.Bacc("TRN2", target_bir_lowering=False, num_devices=1)
    arrays, args = {}, []
    for name, v in laid.items():
        v = _np.ascontiguousarray(v)
        arrays[f"in_{name}_dram"] = v
        args.append(nc.dram_tensor(f"in_{name}_dram", v.shape, _mybir.dt.from_np(v.dtype), kind="ExternalInput").ap())
    fp32 = _mybir.dt.float32
    args.append(nc.dram_tensor("kpad", (h, 2 * l), fp32, kind="Internal").ap())
    args.append(nc.dram_tensor("gates", (experts, t), fp32, kind="Internal").ap())
    args.append(nc.dram_tensor("y_dram", (b, h, l), fp32, kind="Internal").ap())
    args.append(nc.dram_tensor("out_0_dram", (128, t), fp32, kind="ExternalOutput").ap())
    s4d_moe_ffn_decoder(nc, *args)
    r = _run(nc, [arrays], core_ids=[0])
    got = r.results[0]["out_0_dram"]
    return got.reshape(128, t // 128, h).transpose(1, 0, 2).reshape(b, l, h)
```
